# Optimizing a Trainium2 kernel written in Bass

```python
import numpy as np
import jax
import jax.numpy as jnp

def _softmax(x, axis=-1):
    return jax.nn.softmax(x, axis=axis)
def _gelu(x):
    return jax.nn.gelu(x, approximate=True)
def _silu(x):
    return jax.nn.silu(x)
def _sigmoid(x):
    return jax.nn.sigmoid(x)
def _layernorm(x, axis=-1, eps=1e-5):
    m = jnp.mean(x, axis=axis, keepdims=True)
    v = jnp.var(x, axis=axis, keepdims=True)
    return (x - m) / jnp.sqrt(v + eps)
def _scatter_add(tgt, idx, src, axis=0):
    return tgt.at[idx].add(src)
def _segment_sum(src, seg, n):
    return jax.ops.segment_sum(src, seg, n)

kernel_name = 'mk_adj_ffn_d2_adj_256_ab113b'

def setup_inputs(seed: int = 0):
    np.random.seed(seed)
    _w = jnp.asarray
    def _rec_inputs():
        import jax
        import jax.numpy as jnp
        _gk = jax.random.key(seed)
        x = 7.22e-05 + 1 * jax.random.normal(jax.random.fold_in(_gk, 1), (128, 128, 256), jnp.float32)
        _a = jax.random.bernoulli(jax.random.fold_in(_gk, 2), 0.0625, (128, 128, 128))
        _a = jnp.logical_or(_a, jnp.eye(128, dtype=bool))
        _af = _a.astype(jnp.float32)
        _af = _af * jax.random.uniform(jax.random.fold_in(_gk, 3), (128, 128, 128), jnp.float32, 0.05, 1)
        adj = _af
        return x, adj
    x, adj = _rec_inputs()
    def _L0_gnn_setup():
        import jax, jax.numpy as jnp
        import numpy as np
        D_IN = 256
        D_HID = 512
        key = jax.random.key(seed)
        k1, k2, k3, k4, k5, k6 = jax.random.split(key, 6)
        x = jax.random.normal(k1, (8, 4096, D_IN), dtype=jnp.float32)
        adj = jax.random.uniform(k2, (8, 4096, 4096), dtype=jnp.float32)
        s1 = 1.0 / np.sqrt(D_IN)
        s2 = 1.0 / np.sqrt(D_HID)
        W1 = jax.random.uniform(k3, (D_IN, D_HID), dtype=jnp.float32, minval=-s1, maxval=s1)
        b1 = jax.random.uniform(k4, (D_HID,), dtype=jnp.float32, minval=-s1, maxval=s1)
        W2 = jax.random.uniform(k5, (D_HID, D_IN), dtype=jnp.float32, minval=-s2, maxval=s2)
        b2 = jax.random.uniform(k6, (D_IN,), dtype=jnp.float32, minval=-s2, maxval=s2)
        eps = jnp.zeros((1,), dtype=jnp.float32)
        return {'x': x, 'adj': adj, 'eps': eps, 'W1': W1, 'b1': b1, 'W2': W2, 'b2': b2}
    _L0_gnn_all = _L0_gnn_setup()
    _L0_gnn_in = {k: v for k, v in _L0_gnn_all.items() if k in ('eps', 'W1', 'b1', 'W2', 'b2', )}
    del _L0_gnn_all

    def _L0_ffn_setup():
        import math
        import jax, jax.numpy as jnp
        import numpy as np
        CAPACITY_FACTOR = 1.25
        key = jax.random.key(seed)
        ks = jax.random.split(key, 5)
        B, L, D, F, E = (8, 8192, 256, 1024, 8)
        h = jax.random.normal(ks[0], (B, L, D), dtype=jnp.float32)
        gate_w = jax.random.normal(ks[1], (D, E), dtype=jnp.float32) * 0.02
        gate_b = jnp.zeros((E,), dtype=jnp.float32)
        w1 = jax.random.normal(ks[2], (E, D, F), dtype=jnp.float32) * (1.0 / math.sqrt(D))
        b1 = jnp.zeros((E, F), dtype=jnp.float32)
        w2 = jax.random.normal(ks[3], (E, F, D), dtype=jnp.float32) * (1.0 / math.sqrt(F))
        b2 = jnp.zeros((E, D), dtype=jnp.float32)
        return {'h': h, 'gate_w': gate_w, 'gate_b': gate_b, 'w1': w1, 'b1': b1, 'w2': w2, 'b2': b2}
    _L0_ffn_all = _L0_ffn_setup()
    _L0_ffn_in = {k: v for k, v in _L0_ffn_all.items() if k in ('gate_w', 'gate_b', 'w1', 'b1', 'w2', 'b2', )}
    del _L0_ffn_all

    def _L1_gnn_setup():
        import jax, jax.numpy as jnp
        import numpy as np
        B, N, D, H = (8, 2048, 256, 1024)
        RMS_EPS = 1e-06

        def _rmsnorm(h, w, eps=RMS_EPS):
            var = jnp.mean(jnp.square(h), axis=-1, keepdims=True)
            return h * jax.lax.rsqrt(var + eps) * w
        key = jax.random.key(seed)
        ks = jax.random.split(key, 5)
        x = jax.random.normal(ks[0], (B, N, D), dtype=jnp.float32)
        adjacency = jax.random.uniform(ks[1], (B, N, N), dtype=jnp.float32)
        epsilon = jnp.zeros((), dtype=jnp.float32)
        W1 = jax.random.normal(ks[2], (D, H), dtype=jnp.float32) * (1.0 / np.sqrt(D))
        b1 = jnp.zeros((H,), dtype=jnp.float32)
        rms_weight = jnp.ones((H,), dtype=jnp.float32)
        W2 = jax.random.normal(ks[3], (H, D), dtype=jnp.float32) * (1.0 / np.sqrt(H))
        b2 = jnp.zeros((D,), dtype=jnp.float32)
        return {'x': x, 'adjacency': adjacency, 'epsilon': epsilon, 'W1': W1, 'b1': b1, 'rms_weight': rms_weight, 'W2': W2, 'b2': b2}
    _L1_gnn_all = _L1_gnn_setup()
    _L1_gnn_in = {k: v for k, v in _L1_gnn_all.items() if k in ('epsilon', 'W1', 'b1', 'rms_weight', 'W2', 'b2', )}
    del _L1_gnn_all

    def _L1_ffn_setup():
        import jax, jax.numpy as jnp
        import numpy as np
        D = 256
        E = 4
        C = 4
        DC = 64
        H = 2
        DH = DC // H
        EPS = 1e-05
        key = jax.random.key(seed)
        ks = jax.random.split(key, 8)
        B, T = (4, 1024)
        s = 0.02
        return {'x': jax.random.normal(ks[0], (B, T, D), dtype=jnp.float32), 'norm_w': jnp.ones((D,), dtype=jnp.float32), 'router_w': jax.random.normal(ks[1], (E, D), dtype=jnp.float32) * s, 'router_b': jnp.zeros((E,), dtype=jnp.float32), 'qkv_w': jax.random.normal(ks[2], (E, 3 * DC, DC), dtype=jnp.float32) * s, 'proj_w': jax.random.normal(ks[3], (E, DC, DC), dtype=jnp.float32) * s, 'proj_b': jnp.zeros((E, DC), dtype=jnp.float32), 'out_w': jax.random.normal(ks[4], (D, D), dtype=jnp.float32) * s}
    _L1_ffn_all = _L1_ffn_setup()
    _L1_ffn_in = {k: v for k, v in _L1_ffn_all.items() if k in ('norm_w', 'router_w', 'router_b', 'qkv_w', 'proj_w', 'proj_b', 'out_w', )}
    del _L1_ffn_all

    return {
        "x": x,
        "adj": adj,
        "L0_gnn_eps": _L0_gnn_in["eps"],
        "L0_gnn_W1": _L0_gnn_in["W1"],
        "L0_gnn_b1": _L0_gnn_in["b1"],
        "L0_gnn_W2": _L0_gnn_in["W2"],
        "L0_gnn_b2": _L0_gnn_in["b2"],
        "L0_ffn_gate_w": _L0_ffn_in["gate_w"],
        "L0_ffn_gate_b": _L0_ffn_in["gate_b"],
        "L0_ffn_w1": _L0_ffn_in["w1"],
        "L0_ffn_b1": _L0_ffn_in["b1"],
        "L0_ffn_w2": _L0_ffn_in["w2"],
        "L0_ffn_b2": _L0_ffn_in["b2"],
        "L1_gnn_epsilon": _L1_gnn_in["epsilon"],
        "L1_gnn_W1": _L1_gnn_in["W1"],
        "L1_gnn_b1": _L1_gnn_in["b1"],
        "L1_gnn_rms_weight": _L1_gnn_in["rms_weight"],
        "L1_gnn_W2": _L1_gnn_in["W2"],
        "L1_gnn_b2": _L1_gnn_in["b2"],
        "L1_ffn_norm_w": _L1_ffn_in["norm_w"],
        "L1_ffn_router_w": _L1_ffn_in["router_w"],
        "L1_ffn_router_b": _L1_ffn_in["router_b"],
        "L1_ffn_qkv_w": _L1_ffn_in["qkv_w"],
        "L1_ffn_proj_w": _L1_ffn_in["proj_w"],
        "L1_ffn_proj_b": _L1_ffn_in["proj_b"],
        "L1_ffn_out_w": _L1_ffn_in["out_w"],
    }

def reference(x, adj, L0_gnn_eps, L0_gnn_W1, L0_gnn_b1, L0_gnn_W2, L0_gnn_b2, L0_ffn_gate_w, L0_ffn_gate_b, L0_ffn_w1, L0_ffn_b1, L0_ffn_w2, L0_ffn_b2, L1_gnn_epsilon, L1_gnn_W1, L1_gnn_b1, L1_gnn_rms_weight, L1_gnn_W2, L1_gnn_b2, L1_ffn_norm_w, L1_ffn_router_w, L1_ffn_router_b, L1_ffn_qkv_w, L1_ffn_proj_w, L1_ffn_proj_b, L1_ffn_out_w):
    import jax
    import jax.numpy as jnp
    def _L0_gnn_ref(x, adj, eps, W1, b1, W2, b2):
        import jax, jax.numpy as jnp
        import numpy as np
        D_IN = 256
        D_HID = 512
        aggregated = jnp.einsum('bnm,bmd->bnd', adj, x)
        h = (1.0 + eps) * x + aggregated
        h = jax.nn.relu(h @ W1 + b1)
        return h @ W2 + b2

    def _L0_ffn_ref(h, gate_w, gate_b, w1, b1, w2, b2):
        import math
        import jax, jax.numpy as jnp
        import numpy as np
        CAPACITY_FACTOR = 1.25
        B, L, D = h.shape
        E = gate_w.shape[1]
        T = B * L
        C = max(1, math.ceil(CAPACITY_FACTOR * T / E))
        x = h.reshape(T, D)
        logits = x @ gate_w + gate_b
        probs = jax.nn.softmax(logits, axis=-1)
        idx = jnp.argmax(probs, axis=-1)
        prb = jnp.take_along_axis(probs, idx[:, None], axis=1)[:, 0]
        one_hot = jax.nn.one_hot(idx, E, dtype=jnp.float32)
        pos = (jnp.cumsum(one_hot, axis=0) * one_hot).sum(-1).astype(jnp.int32) - 1
        kept = pos < C
        pos_safe = jnp.where(kept, pos, C)
        buf = jnp.zeros((E, C, D), dtype=h.dtype).at[idx, pos_safe].set(x, mode='drop')
        hmid = jax.nn.relu(jnp.einsum('ecd,edf->ecf', buf, w1) + b1[:, None, :])
        ybuf = jnp.einsum('ecf,efd->ecd', hmid, w2) + b2[:, None, :]
        pos_g = jnp.minimum(pos, C - 1)
        y_tok = ybuf[idx, pos_g] * (prb * kept)[:, None]
        y = y_tok.reshape(B, L, D)
        y = jnp.nan_to_num(y, nan=0.0, posinf=10000.0, neginf=-10000.0)
        return y

    def _L1_gnn_ref(x, adjacency, epsilon, W1, b1, rms_weight, W2, b2):
        import jax, jax.numpy as jnp
        import numpy as np
        B, N, D, H = (8, 2048, 256, 1024)
        RMS_EPS = 1e-06

        def _rmsnorm(h, w, eps=RMS_EPS):
            var = jnp.mean(jnp.square(h), axis=-1, keepdims=True)
            return h * jax.lax.rsqrt(var + eps) * w
        neighbor_sum = jnp.einsum('bnm,bmd->bnd', adjacency, x)
        agg = epsilon * x + neighbor_sum
        h = jnp.einsum('bnd,dh->bnh', agg, W1) + b1
        h = jax.nn.silu(_rmsnorm(h, rms_weight))
        out = jnp.einsum('bnh,hd->bnd', h, W2) + b2
        return out

    def _L1_ffn_ref(x, norm_w, router_w, router_b, qkv_w, proj_w, proj_b, out_w):
        import jax, jax.numpy as jnp
        import numpy as np
        D = 256
        E = 4
        C = 4
        DC = 64
        H = 2
        DH = DC // H
        EPS = 1e-05
        B, T, _ = x.shape
        residual = x
        mean = jnp.mean(x, axis=-1, keepdims=True)
        var = jnp.mean((x - mean) ** 2, axis=-1, keepdims=True)
        xn = (x - mean) / jnp.sqrt(var + EPS) * norm_w
        gate = jax.nn.softmax(xn @ router_w.T + router_b, axis=-1)
        xc = xn.reshape(B, T, C, DC)
        qkv = jnp.einsum('btcd,ekd->btcek', xc, qkv_w)
        qkv = qkv.reshape(B, T, C, E, 3, H, DH)
        qkv = qkv.transpose(4, 0, 2, 3, 5, 1, 6)
        q, k, v = (qkv[0], qkv[1], qkv[2])
        scale = 1.0 / np.sqrt(DH).astype(np.float32)
        attn = jnp.einsum('bcehtd,bcehsd->bcehts', q, k) * scale
        attn = jax.nn.softmax(attn, axis=-1)
        y = jnp.einsum('bcehts,bcehsd->bcehtd', attn, v)
        y = y.transpose(0, 4, 1, 2, 3, 5).reshape(B, T, C, E, DC)
        y = jnp.einsum('btced,eod->btceo', y, proj_w) + proj_b[None, None, None, :, :]
        out = jnp.einsum('btceo,bte->btco', y, gate).reshape(B, T, D)
        return residual + out @ out_w.T

    x = x + _L0_gnn_ref(_layernorm(x, axis=-1), adj, L0_gnn_eps, L0_gnn_W1, L0_gnn_b1, L0_gnn_W2, L0_gnn_b2)
    x = x + _L0_ffn_ref(_layernorm(x, axis=-1), L0_ffn_gate_w, L0_ffn_gate_b, L0_ffn_w1, L0_ffn_b1, L0_ffn_w2, L0_ffn_b2)
    x = x + _L1_gnn_ref(_layernorm(x, axis=-1), adj, L1_gnn_epsilon, L1_gnn_W1, L1_gnn_b1, L1_gnn_rms_weight, L1_gnn_W2, L1_gnn_b2)
    x = x + _L1_ffn_ref(_layernorm(x, axis=-1), L1_ffn_norm_w, L1_ffn_router_w, L1_ffn_router_b, L1_ffn_qkv_w, L1_ffn_proj_w, L1_ffn_proj_b, L1_ffn_out_w)
    return x


_drawn_inputs = setup_inputs


def setup_inputs(seed=0):
    import zlib

    import numpy as np

    out = dict(_drawn_inputs(seed))
    spreads = {'L0_ffn_gate_b': (0.0, 0.1),
     'L0_ffn_b1': (0.0, 0.685),
     'L0_ffn_b2': (0.0, 0.484),
     'L1_gnn_b1': (0.0, 0.314),
     'L1_gnn_rms_weight': (1.0, 0.2),
     'L1_gnn_b2': (0.0, 0.1),
     'L1_ffn_norm_w': (1.0, 0.6),
     'L1_ffn_router_b': (0.0, 0.8),
     'L1_ffn_proj_b': (0.0, 0.8)}
    factors = {'L0_gnn_b1': 3.129,
     'L1_ffn_router_w': 8.0,
     'L1_ffn_qkv_w': 8.0,
     'L1_ffn_proj_w': 8.0,
     'L1_ffn_out_w': 8.0}
    for name, (base, spread) in spreads.items():
        noise = np.random.default_rng([zlib.crc32(name.encode()), seed]).standard_normal(out[name].shape)
        drawn = base * np.exp(spread * noise) if base else spread * noise
        out[name] = jnp.asarray(drawn.astype(out[name].dtype))
    for name, factor in factors.items():
        out[name] = (out[name] * factor).astype(out[name].dtype)
    return out
```

```python
import concourse.bass as bass
from concourse import mybir
from contextlib import ExitStack

F32 = mybir.dt.float32
F32R = mybir.dt.float32r
BF16 = mybir.dt.bfloat16
U32 = mybir.dt.uint32
ALU = mybir.AluOpType
ACT = mybir.ActivationFunctionType
AX = mybir.AxisListType

P = 128
GRAPHS = 128
D = 256
DK = D // P
NU = 4
W = NU * P
G = GRAPHS // NU
T = GRAPHS * P
LN_EPS = 1e-5

H0 = 512
E0 = 8
F0 = 1024
CAP = -(-5 * T // (4 * E0))
SG = CAP // W
SLOTS = E0 * CAP

H1 = 1024
RMS_EPS = 1e-6

E1 = 4
C1 = 4
DC = 64
NH = 2
DH = DC // NH
EH = E1 * NH
CH = C1 * NH
EPS1 = 1e-5
SCALE = float(1.0 / (DH ** 0.5))
CLAMP = 10000.0

LEAD = 2


class Count:

    def __init__(self, ctx, nc, name, n=1):
        self.sem, self.n = ctx.enter_context(nc.semaphore(name)), n

    def start(self, eng):
        eng.sem_inc(self.sem, LEAD * self.n)

    def at(self, g, k):
        return (g.n + LEAD) * self.n + k

    def done(self, g, back=0):
        return (g.n + (LEAD + 1 - back)) * self.n


class Arrivals:

    def __init__(self, ctx, nc, name, n=16):
        self.sems, self.n = [ctx.enter_context(nc.semaphore(f"{name}{u}")) for u in range(2)], n

    def wait(self, eng, g, back=0):
        eng.wait_ge(self.sems[g.u], (g.h * (g.span // 2) + g.k // 2 + 1 - back // 2) * self.n)


class Group:

    def __init__(self, h, k, span=2, left=None):
        self.h, self.k, self.span = h, k, span
        self.n, self.u = h * span + k, k % 2
        self.final = left is not None and left < 2
        self.last = left == 0

    def _ahead(self, by):
        h, k = self.h + (self.k + by) // self.span, (self.k + by) % self.span
        return Group(h, k, self.span)

    def next(self):
        return self._ahead(1)

    def after_next(self):
        return self._ahead(2)

    def of(self, view):
        if isinstance(self.h, int):
            return view[self.h, self.k]
        part = view[bass.ds(self.h, 1), self.k]
        axes = " ".join("bcdefg"[:len(part.shape) - 2])
        return part.rearrange(f"a p {axes} -> (a p) {axes}")


def groups(eng, count, body, span=2):
    with eng.Fori(0, count // span - 1) as h:
        for k in range(span):
            body(Group(h, k, span))
    for k in range(span):
        body(Group(count // span - 1, k, span, left=span - 1 - k))


def by_tokens(ap):
    return ap.rearrange("(h two u p) d -> h two p u d", two=2, u=NU, p=P)


def graph_block_0(nc, io, dram, keep):
    with ExitStack() as ctx:
        def sb(name, shape, dt=F32):
            return ctx.enter_context(nc.sbuf_tensor("a_" + name, shape, dt))

        def pb(name, shape, dt=F32):
            return ctx.enter_context(nc.psum_tensor("a_" + name, shape, dt))

        def count(name, n=1):
            return Count(ctx, nc, "a_" + name, n)

        def arrivals(name, n):
            return Arrivals(ctx, nc, "a_" + name, n)

        w1 = sb("w1", [P, DK, H0])
        w2 = sb("w2", [P, H0 // P, D])
        b1 = sb("b1", [P, H0 // P])
        b2 = sb("b2", [P, D])
        gw = sb("gw", [P, DK, E0])
        gb = sb("gb", [P, E0])
        eps = sb("eps", [P, 1])
        eye1 = sb("eye1", [P, P])
        ident = sb("ident", [P, P])
        tri = sb("tri", [P, P])
        trib = sb("trib", [P, P], BF16)
        onesb = sb("onesb", [P, P], BF16)
        iota_e = sb("iota_e", [P, E0])
        tok = sb("tok", [P, NU])
        half = sb("half", [P, NU])
        epst = sb("epst", [P, NU])

        x = [sb(f"x{u}", [P, NU, D]) for u in range(2)]
        adj = [sb(f"adj{u}", [P, NU, P]) for u in range(2)]
        xn = [sb(f"xn{u}", [P, NU, D]) for u in range(2)]
        hT = [sb(f"hT{u}", [P, DK, W]) for u in range(2)]
        mid = [sb(f"mid{u}", [P, H0 // P, W]) for u in range(2)]
        x1 = [sb(f"x1{u}", [P, NU, D]) for u in range(2)]
        x1n = [sb(f"x1n{u}", [P, NU, D]) for u in range(2)]
        x1T = [sb(f"x1T{u}", [P, DK, W]) for u in range(2)]
        stats = sb("stats", [P, NU, 6])
        mv = sb("mv", [P, NU, 2])
        rs = sb("rs", [P, NU])
        stats1 = sb("stats1", [P, NU, 6])
        mv1 = sb("mv1", [P, NU, 2])
        rs1 = sb("rs1", [P, NU])
        lg = sb("lg", [P, NU, E0])
        mx = sb("mx", [P, NU])
        dl = sb("dl", [P, NU, E0])
        ex = sb("ex", [P, NU, E0])
        se = sb("se", [P, NU])
        prob = sb("prob", [P, NU])
        eq = sb("eq", [P, NU, E0])
        cand = sb("cand", [P, NU, E0])
        first = sb("first", [P, NU])
        oh = sb("oh", [P, NU, E0])
        ohb = sb("ohb", [P, NU, E0], BF16)
        seen = sb("seen", [P, NU + 1, E0])
        seenb = sb("seenb", [P, NU, E0], BF16)
        rank = sb("rank", [P, NU, E0])
        pos = sb("pos", [P, NU])
        kept = sb("kept", [P, NU])
        base = sb("base", [P, NU])
        slot = sb("slot", [P, NU])
        over = sb("over", [P, NU])
        capped = sb("capped", [P, NU])
        slot_i = [sb(f"slot_i{u}", [P, NU], U32) for u in range(2)]
        tok_i = [sb(f"tok_i{u}", [P, NU], U32) for u in range(2)]

        hp = [pb(f"hp{k}", [P, W]) for k in range(DK)]
        mp = [pb(f"mp{k}", [P, W]) for k in range(2)]
        yp = [pb(f"yp{k}", [P, 2, D]) for k in range(2)]
        lp = pb("lp", [P, NU, E0])
        rp = pb("rp", [P, NU, E0])

        consts = ctx.enter_context(nc.semaphore("a_consts"))
        setup = ctx.enter_context(nc.semaphore("a_setup"))
        zero_in = ctx.enter_context(nc.semaphore("a_zero_in"))
        x_in = arrivals("x_in", 16)
        adj_in = arrivals("adj_in", 16)
        st_ok, st1_ok = count("st_ok"), count("st1_ok")
        mv_ok, mv1_ok = count("mv_ok"), count("mv1_ok")
        var_ok, var1_ok = count("var_ok"), count("var1_ok")
        rs_ok, rs1_ok = count("rs_ok"), count("rs1_ok")
        xn_ok = count("xn_ok")
        adj_ok = count("adj_ok")
        xb_ok = count("xb_ok")
        hp_ok = count("hp_ok")
        hT_ok = count("hT_ok")
        tr_ok = count("tr_ok")
        x1T_ok = count("x1T_ok")
        mp_ok = count("mp_ok", H0 // P)
        mid_ok = count("mid_ok", H0 // P)
        yp_ok = count("yp_ok", 2)
        x1_ok = count("x1_ok")
        x1n_ok = count("x1n_ok")
        x1_out = arrivals("x1_out", 32)
        lp_ok = count("lp_ok")
        lg_ok = count("lg_ok", 3)
        ex_ok = count("ex_ok")
        oh_ok = count("oh_ok", 5)
        sn_ok = count("sn_ok", NU + 2)
        rp_ok = count("rp_ok")
        sl_ok = count("sl_ok", 9)
        ids_ok = count("ids_ok")
        tab_out = arrivals("tab_out", 16 * NU)
        passed = ctx.enter_context(nc.semaphore("a_passed"))
        pool_passed = ctx.enter_context(nc.semaphore("a_pool_passed"))
        block = ctx.enter_context(nc.Block())

        xv, av, x1v, x1nv = (by_tokens(io["x"]), by_tokens(io["adjT"]), by_tokens(dram["x1"]),
                             by_tokens(dram["x1n"]))
        N_CONST = 12

        def g_cols(g):
            return slice(g.n * NU, g.n * NU + NU) if isinstance(g.n, int) else bass.ds(g.n * NU, NU)

        @block.sync
        def _(sp):
            for dst, src in ((w1[:, :, :], io["W1a"].rearrange("(k p) f -> p k f", p=P)),
                             (w2[:, :, :], io["W2a"].rearrange("(k p) f -> p k f", p=P)),
                             (b1[:, :], io["b1a"]), (b2[:, :], io["b2a"]),
                             (gw[:, :, :], io["gate_w"].rearrange("(k p) e -> p k e", p=P)),
                             (gb[:, :], io["gate_b"]), (eps[:, :], io["eps0"]), (ident[:, :], io["ident"]),
                             (tri[:, :], io["tri"]), (iota_e[:, :], io["iota_e"]), (tok[:, :], io["tok"])):
                sp.dma_start(dst, src).then_inc(consts, 16)
            sp.dma_start(dram["slot_token"].rearrange("(p n) a -> p (n a)", p=P), io["no_token"])\
              .then_inc(zero_in, 16)

            def load(g):
                sp.wait_ge(x1_ok.sem, x1_ok.done(g, 2))
                sp.dma_start(x[g.u][:, :, :], g.of(xv)).then_inc(x_in.sems[g.u], 16)
                sp.wait_ge(hp_ok.sem, hp_ok.done(g, 2))
                sp.dma_start(adj[g.u][:, :, :], g.of(av)).then_inc(adj_in.sems[g.u], 16)

            def body(g):
                sp.wait_ge(x1_ok.sem, x1_ok.done(g))
                sp.dma_start(g.of(x1v), x1[g.u][:, :, :]).then_inc(x1_out.sems[g.u], 16)
                if not g.final:
                    load(g.after_next())
                sp.wait_ge(x1n_ok.sem, x1n_ok.done(g))
                sp.dma_start(g.of(x1nv), x1n[g.u][:, :, :]).then_inc(x1_out.sems[g.u], 16)

            load(Group(0, 0))
            load(Group(0, 1))
            groups(sp, G, body)
            for u in range(2):
                x1_out.wait(sp, Group(G // 2 - 1, u))
            sp.wait_ge(zero_in, 16)

        @block.vector
        def _(dve):
            for c in (st_ok, mv_ok, st1_ok, mv1_ok, xn_ok, adj_ok, x1_ok, x1n_ok, lg_ok, oh_ok, sn_ok, sl_ok):
                c.start(dve)
            dve.wait_ge(consts, 16 * (N_CONST - 1))
            nc.vector.memset(half[:, :], -0.5).then_inc(setup, 1)
            nc.vector.memset(epst[:, :], LN_EPS).then_inc(setup, 1)
            nc.vector.memset(onesb[:, :], 1.0).then_inc(setup, 1)
            nc.vector.memset(seen[:, :, :], 0.0).then_inc(setup, 1)
            nc.vector.tensor_scalar(eps[:, :], eps[:, :], 1.0, None, ALU.add).then_inc(setup, 1)
            nc.vector.tensor_copy(trib[:, :], tri[:, :]).then_inc(setup, 1)
            dve.wait_ge(setup, 6)
            nc.vector.tensor_scalar(eye1[:, :], ident[:, :], eps[:, :], None, ALU.mult).then_inc(setup, 1)
            dve.wait_ge(setup, 7)

            def statistics(src, st, mvt, g, st_ok, mv_ok):
                for t in range(NU):
                    last = nc.vector.bn_stats(st[:, t, :], src[:, t, :])
                last.then_inc(st_ok.sem, 1)
                dve.wait_ge(st_ok.sem, st_ok.done(g))
                dve.sem_inc(passed, 1)
                for t in range(NU):
                    last = nc.vector.bn_aggr(mvt[:, t, :], st[:, t, :])
                last.then_inc(mv_ok.sem, 1)

            def normalise(dst, src, mvt, rst):
                for t in range(NU):
                    last = nc.vector.tensor_scalar(dst[:, t, :], src[:, t, :], mvt[:, t, 0:1], rst[:, t:t + 1],
                                                   ALU.subtract, ALU.mult)
                return last

            def prepare(g):
                x_in.wait(dve, g)
                statistics(x[g.u], stats, mv, g, st_ok, mv_ok)
                adj_in.wait(dve, g)
                nc.vector.tensor_tensor(adj[g.u][:, :, :], adj[g.u][:, :, :],
                                        eye1[:, :].rearrange("p (a q) -> p a q", a=1).to_broadcast([P, NU, P]),
                                        ALU.add).then_inc(adj_ok.sem, 1)
                dve.wait_ge(rs_ok.sem, rs_ok.done(g))
                dve.wait_ge(hp_ok.sem, hp_ok.done(g, 2))
                normalise(xn[g.u], x[g.u], mv, rs).then_inc(xn_ok.sem, 1)

            def body(g):
                dve.wait_ge(xb_ok.sem, xb_ok.done(g))
                x1_out.wait(dve, g, 2)
                for t in range(2):
                    dve.wait_ge(yp_ok.sem, yp_ok.at(g, t + 1))
                    last = nc.vector.tensor_tensor(x1[g.u][:, 2 * t:2 * t + 2, :], yp[t][:, :, :],
                                                   x[g.u][:, 2 * t:2 * t + 2, :], ALU.add)
                last.then_inc(x1_ok.sem, 1)
                dve.wait_ge(x1_ok.sem, x1_ok.done(g))
                statistics(x1[g.u], stats1, mv1, g, st1_ok, mv1_ok)
                dve.wait_ge(rs1_ok.sem, rs1_ok.done(g))
                x1_out.wait(dve, g, 2)
                dve.wait_ge(tr_ok.sem, tr_ok.done(g, 2))
                normalise(x1n[g.u], x1[g.u], mv1, rs1).then_inc(x1n_ok.sem, 1)
                dve.wait_ge(lp_ok.sem, lp_ok.done(g))
                nc.vector.tensor_tensor(lg[:, :, :], lp[:, :, :],
                                        gb[:, :].rearrange("p (a e) -> p a e", a=1).to_broadcast([P, NU, E0]),
                                        ALU.add).then_inc(lg_ok.sem, 1)
                dve.wait_ge(lg_ok.sem, lg_ok.at(g, 1))
                nc.vector.tensor_reduce(mx[:, :], lg[:, :, :], AX.X, ALU.max).then_inc(lg_ok.sem, 1)
                dve.wait_ge(lg_ok.sem, lg_ok.at(g, 2))
                mxb = mx[:, :].rearrange("p (u a) -> p u a", a=1).to_broadcast([P, NU, E0])
                nc.vector.tensor_tensor(dl[:, :, :], lg[:, :, :], mxb, ALU.subtract).then_inc(lg_ok.sem, 1)
                nc.vector.tensor_tensor(eq[:, :, :], lg[:, :, :], mxb, ALU.is_equal).then_inc(oh_ok.sem, 1)
                ieb = iota_e[:, :].rearrange("p (a e) -> p a e", a=1).to_broadcast([P, NU, E0])
                dve.wait_ge(oh_ok.sem, oh_ok.at(g, 1))
                nc.vector.scalar_tensor_tensor(cand[:, :, :], eq[:, :, :], -float(E0), ieb, ALU.mult, ALU.add)\
                  .then_inc(oh_ok.sem, 1)
                dve.wait_ge(oh_ok.sem, oh_ok.at(g, 2))
                nc.vector.tensor_reduce(first[:, :], cand[:, :, :], AX.X, ALU.min).then_inc(oh_ok.sem, 1)
                dve.wait_ge(oh_ok.sem, oh_ok.at(g, 3))
                nc.vector.tensor_tensor(oh[:, :, :], cand[:, :, :],
                                        first[:, :].rearrange("p (u a) -> p u a", a=1).to_broadcast([P, NU, E0]),
                                        ALU.is_equal).then_inc(oh_ok.sem, 1)
                dve.wait_ge(oh_ok.sem, oh_ok.at(g, 4))
                dve.wait_ge(rp_ok.sem, rp_ok.done(g, 1))
                nc.vector.tensor_copy(ohb[:, :, :], oh[:, :, :]).then_inc(oh_ok.sem, 1)
                nc.vector.tensor_copy(seen[:, 0, :], seen[:, NU, :]).then_inc(sn_ok.sem, 1)
                for t in range(NU):
                    dve.wait_ge(sn_ok.sem, sn_ok.at(g, t + 1))
                    nc.vector.tensor_tensor(seen[:, t + 1, :], seen[:, t, :], oh[:, t, :], ALU.add)\
                      .then_inc(sn_ok.sem, 1)
                dve.wait_ge(sn_ok.sem, sn_ok.at(g, NU + 1))
                nc.vector.tensor_copy(seenb[:, :, :], seen[:, 0:NU, :]).then_inc(sn_ok.sem, 1)
                if not g.final:
                    prepare(g.after_next())
                dve.wait_ge(ex_ok.sem, ex_ok.done(g))
                nc.vector.tensor_reduce(se[:, :], ex[:, :, :], AX.X, ALU.add).then_inc(sl_ok.sem, 1)
                dve.wait_ge(sl_ok.sem, sl_ok.at(g, 1))
                nc.vector.reciprocal(prob[:, :], se[:, :]).then_inc(sl_ok.sem, 1)
                dve.wait_ge(rp_ok.sem, rp_ok.done(g))
                nc.vector.tensor_tensor(rank[:, :, :], rp[:, :, :], oh[:, :, :], ALU.mult).then_inc(sl_ok.sem, 1)
                dve.wait_ge(sl_ok.sem, sl_ok.at(g, 3))
                nc.vector.tensor_reduce(pos[:, :], rank[:, :, :], AX.X, ALU.add)
                nc.vector.tensor_scalar(base[:, :], first[:, :], float(CAP), float(SLOTS - 1), ALU.mult, ALU.add)\
                  .then_inc(sl_ok.sem, 1)
                dve.wait_ge(sl_ok.sem, sl_ok.at(g, 4))
                nc.vector.tensor_scalar(kept[:, :], pos[:, :], float(CAP), None, ALU.is_le)
                nc.vector.tensor_scalar(capped[:, :], pos[:, :], float(CAP), None, ALU.min)
                nc.vector.tensor_scalar(over[:, :], tok[:, :], 1.0, float(SLOTS), ALU.mult, ALU.add)\
                  .then_inc(sl_ok.sem, 1)
                dve.wait_ge(sl_ok.sem, sl_ok.at(g, 5))
                nc.vector.tensor_tensor(keep["slot"][:, g_cols(g)], base[:, :], capped[:, :], ALU.add)
                nc.vector.tensor_tensor(keep["gate"][:, g_cols(g)], prob[:, :], kept[:, :], ALU.mult)
                nc.vector.tensor_tensor(slot[:, :], base[:, :], pos[:, :], ALU.add)\
                  .then_inc(sl_ok.sem, 1)
                dve.wait_ge(sl_ok.sem, sl_ok.at(g, 6))
                nc.vector.tensor_tensor(slot[:, :], slot[:, :], over[:, :], ALU.subtract).then_inc(sl_ok.sem, 1)
                dve.wait_ge(sl_ok.sem, sl_ok.at(g, 7))
                nc.vector.tensor_tensor(slot[:, :], slot[:, :], kept[:, :], ALU.mult).then_inc(sl_ok.sem, 1)
                dve.wait_ge(sl_ok.sem, sl_ok.at(g, 8))
                tab_out.wait(dve, g, 2)
                nc.vector.tensor_tensor(slot_i[g.u][:, :], slot[:, :], over[:, :], ALU.add)
                nc.vector.tensor_copy(tok_i[g.u][:, :], tok[:, :]).then_inc(sl_ok.sem, 1)
                dve.wait_ge(sl_ok.sem, sl_ok.done(g))
                nc.vector.tensor_scalar(tok[:, :], tok[:, :], float(W), None, ALU.add).then_inc(setup, 1)
                dve.wait_ge(setup, g.n + 8)

            prepare(Group(0, 0))
            prepare(Group(0, 1))
            groups(dve, G, body)

        @block.gpsimd
        def _(pool):
            for c in (var_ok, rs_ok, var1_ok, rs1_ok, xb_ok):
                c.start(pool)
            pool.wait_ge(setup, 7)
            pool.wait_ge(zero_in, 16)

            def inverse_root(dst, mvt, g, mv_ok, var_ok, rs_ok):
                pool.wait_ge(mv_ok.sem, mv_ok.done(g))
                pool.wait_ge(xn_ok.sem, xn_ok.done(g, 1))
                pool.wait_ge(x1n_ok.sem, x1n_ok.done(g, 2))
                nc.gpsimd.tensor_tensor(dst[:, :], mvt[:, :, 1], epst[:, :], ALU.add).then_inc(var_ok.sem, 1)
                pool.wait_ge(var_ok.sem, var_ok.done(g))
                nc.gpsimd.tensor_tensor(dst[:, :], dst[:, :], half[:, :], ALU.pow).then_inc(rs_ok.sem, 1)

            def body(g):
                pool.wait_ge(xn_ok.sem, xn_ok.done(g))
                nc.gpsimd.tensor_tensor(x[g.u][:, :, :], x[g.u][:, :, :],
                                        b2[:, :].rearrange("p (a d) -> p a d", a=1).to_broadcast([P, NU, D]),
                                        ALU.add).then_inc(xb_ok.sem, 1)
                inverse_root(rs1, mv1, g, mv1_ok, var1_ok, rs1_ok)
                if not g.final:
                    inverse_root(rs, mv, g.after_next(), mv_ok, var_ok, rs_ok)
                pool.wait_ge(sl_ok.sem, sl_ok.done(g))
                pool.sem_inc(pool_passed, 1)
                for t in range(NU):
                    nc.gpsimd.indirect_dma_start(
                        out=dram["slot_token"],
                        out_offset=bass.IndirectOffsetOnAxis(ap=slot_i[g.u][:, t:t + 1], axis=0),
                        in_=tok_i[g.u][:, t:t + 1], in_offset=None).then_inc(tab_out.sems[g.u], 16)

            for u in range(2):
                inverse_root(rs, mv, Group(0, u), mv_ok, var_ok, rs_ok)
            groups(pool, G, body)
            for u in range(2):
                tab_out.wait(pool, Group(G // 2 - 1, u))

        @block.scalar
        def _(act):
            for c in (hT_ok, mid_ok, ex_ok, x1T_ok):
                c.start(act)
            act.wait_ge(consts, 16 * (N_CONST - 1))

            def mlp(g):
                act.wait_ge(hp_ok.sem, hp_ok.done(g))
                act.wait_ge(mp_ok.sem, mp_ok.done(g, 2))
                for k in range(DK):
                    last = nc.scalar.activation(hT[g.u][:, k, :], hp[k][:, :], ACT.Copy)
                last.then_inc(hT_ok.sem, 1)
                act.wait_ge(yp_ok.sem, yp_ok.done(g, 2))
                for f in range(H0 // P):
                    act.wait_ge(mp_ok.sem, mp_ok.at(g, f + 1))
                    nc.scalar.activation(mid[g.u][:, f, :], mp[f % 2][:, :], ACT.Relu, bias=b1[:, f:f + 1])\
                      .then_inc(mid_ok.sem, 1)

            def body(g):
                if not g.last:
                    mlp(g.next())
                act.wait_ge(tr_ok.sem, tr_ok.done(g))
                act.wait_ge(lp_ok.sem, lp_ok.done(g, 2))
                for k in range(DK):
                    last = nc.scalar.activation(x1T[g.u][:, k, :], hp[k][:, :], ACT.Copy)
                last.then_inc(x1T_ok.sem, 1)
                act.wait_ge(lg_ok.sem, lg_ok.done(g))
                nc.scalar.activation(ex[:, :, :], dl[:, :, :], ACT.Exp).then_inc(ex_ok.sem, 1)

            mlp(Group(0, 0))
            groups(act, G, body)

        @block.tensor
        def _(pe):
            for c in (hp_ok, mp_ok, yp_ok, lp_ok, rp_ok, tr_ok):
                c.start(pe)
            pe.wait_ge(setup, 7)

            def up(g):
                pe.wait_ge(xn_ok.sem, xn_ok.done(g))
                pe.wait_ge(adj_ok.sem, adj_ok.done(g))
                pe.wait_ge(x1T_ok.sem, x1T_ok.done(g, 2))
                pe.wait_ge(hT_ok.sem, hT_ok.done(g, 1))
                for k in range(DK):
                    for t in range(NU):
                        last = nc.tensor.matmul(hp[k][:, t * P:(t + 1) * P], xn[g.u][:, t, k * P:(k + 1) * P],
                                                adj[g.u][:, t, :], start=True, stop=True)
                last.then_inc(hp_ok.sem, 1)
                pe.wait_ge(hT_ok.sem, hT_ok.done(g))
                for f in range(H0 // P):
                    pe.wait_ge(mid_ok.sem, mid_ok.at(g, f - 1))
                    for k in range(DK):
                        last = nc.tensor.matmul(mp[f % 2][:, :], w1[:, k, f * P:(f + 1) * P], hT[g.u][:, k, :],
                                                start=(k == 0), stop=(k == DK - 1))
                    last.then_inc(mp_ok.sem, 1)

            def down(g):
                pe.wait_ge(mid_ok.sem, mid_ok.done(g))
                pe.wait_ge(x1_ok.sem, x1_ok.done(g, 1))
                for t in range(NU):
                    for f in range(H0 // P):
                        last = nc.tensor.matmul(yp[t // 2][:, t % 2, :], mid[g.u][:, f, t * P:(t + 1) * P],
                                                w2[:, f, :], start=(f == 0), stop=(f == H0 // P - 1))
                    if t % 2:
                        last.then_inc(yp_ok.sem, 1)

            def body(g):
                if not g.last:
                    up(g.next())
                pe.wait_ge(x1n_ok.sem, x1n_ok.done(g))
                if not g.last:
                    pe.wait_ge(hT_ok.sem, hT_ok.done(g.next()))
                for k in range(DK):
                    for t in range(NU):
                        last = nc.tensor.transpose(hp[k][:, t * P:(t + 1) * P], x1n[g.u][:, t, k * P:(k + 1) * P],
                                                   ident[:, :])
                last.then_inc(tr_ok.sem, 1)
                pe.wait_ge(x1T_ok.sem, x1T_ok.done(g))
                for t in range(NU):
                    for k in range(DK):
                        last = nc.tensor.matmul(lp[:, t, :], x1T[g.u][:, k, t * P:(t + 1) * P], gw[:, k, :],
                                                start=(k == 0), stop=(k == DK - 1))
                last.then_inc(lp_ok.sem, 1)
                if not g.last:
                    down(g.next())
                pe.wait_ge(sn_ok.sem, sn_ok.done(g))
                nc.tensor.matmul(rp[:, :, :], trib[:, :], ohb[:, :, :], start=True, stop=False)
                nc.tensor.matmul(rp[:, :, :], onesb[:, :], seenb[:, :, :], start=False, stop=True)\
                  .then_inc(rp_ok.sem, 1)

            up(Group(0, 0))
            down(Group(0, 0))
            groups(pe, G, body)


def experts(nc, io, dram):
    with ExitStack() as ctx:
        def sb(name, shape, dt=F32):
            return ctx.enter_context(nc.sbuf_tensor("b_" + name, shape, dt))

        def pb(name, shape, dt=F32):
            return ctx.enter_context(nc.psum_tensor("b_" + name, shape, dt))

        def count(name, n=1):
            return Count(ctx, nc, "b_" + name, n)

        def arrivals(name, n):
            return Arrivals(ctx, nc, "b_" + name, n)

        FT = F0 // P
        SPAN = 2 * SG
        GS = SLOTS // W
        w1 = [sb(f"w1{u}", [P, DK, F0]) for u in range(2)]
        w2 = [sb(f"w2{u}", [P, FT, D]) for u in range(2)]
        b1 = [sb(f"b1{u}", [P, FT]) for u in range(2)]
        b2 = [sb(f"b2{u}", [P, D]) for u in range(2)]
        ident = sb("ident", [P, P])
        ids = [sb(f"ids{u}", [P, NU], U32) for u in range(2)]
        xg = [sb(f"xg{u}", [P, NU, D]) for u in range(2)]
        xT = [sb(f"xT{u}", [P, DK, W]) for u in range(2)]
        mid = [sb(f"mid{u}", [P, FT, W]) for u in range(2)]
        y = [sb(f"y{u}", [P, NU, D]) for u in range(2)]
        tp = [pb(f"tp{k}", [P, W]) for k in range(DK)]
        mp = [pb(f"mp{k}", [P, W]) for k in range(2)]
        yp = [[pb(f"yp{u}{k}", [P, 2, D]) for k in range(2)] for u in range(2)]

        ident_in = ctx.enter_context(nc.semaphore("b_ident_in"))
        w_in = arrivals("w_in", 64)
        ids_in = arrivals("ids_in", 16)
        xg_in = arrivals("xg_in", 16 * NU)
        tr_ok = count("tr_ok")
        xT_ok = count("xT_ok")
        mp_ok = count("mp_ok", FT)
        even_ok = count("even_ok", FT // 2)
        odd_ok = count("odd_ok", FT // 2)
        yp_ok = count("yp_ok", 2)
        y_ok = count("y_ok")
        y_out = arrivals("y_out", 16)
        pool_passed = ctx.enter_context(nc.semaphore("b_pool_passed"))
        block = ctx.enter_context(nc.Block())

        idv = dram["slot_token"][0:SLOTS].rearrange("(h k p u) a -> h k p (u a)", k=SPAN, u=NU, p=P)
        yv = dram["y"].rearrange("(h k p u) d -> h k p u d", k=SPAN, u=NU, p=P)

        def expert(g):
            return Group(g.h, g.k // SG)

        @block.sync
        def _(sp):
            sp.dma_start(ident[:, :], io["ident"]).then_inc(ident_in, 16)

            def weights(e, used):
                if used is not None:
                    sp.wait_ge(y_ok.sem, y_ok.done(used))
                for dst, src in ((w1[e.u][:, :, :], e.of(io["ew1"].rearrange("(h k) (t p) f -> h k p t f", k=2, p=P))),
                                 (b1[e.u][:, :], e.of(io["eb1"].rearrange("(h k) p t -> h k p t", k=2))),
                                 (w2[e.u][:, :, :], e.of(io["ew2"].rearrange("(h k) (t p) d -> h k p t d", k=2, p=P))),
                                 (b2[e.u][:, :], e.of(io["eb2"].rearrange("(h k) p d -> h k p d", k=2)))):
                    sp.dma_start(dst, src).then_inc(w_in.sems[e.u], 16)

            def load(g):
                xg_in.wait(sp, g, 2)
                sp.dma_start(ids[g.u][:, :], g.of(idv)).then_inc(ids_in.sems[g.u], 16)

            def body(g):
                if not g.final:
                    load(g.after_next())
                sp.wait_ge(y_ok.sem, y_ok.done(g))
                sp.dma_start(g.of(yv), y[g.u][:, :, :]).then_inc(y_out.sems[g.u], 16)
                if g.k % SG == SG - 1 and not in_last_turn(g):
                    weights(expert(g).after_next(), g)

            def in_last_turn(g):
                return isinstance(g.h, int)

            weights(Group(0, 0), None)
            load(Group(0, 0))
            load(Group(0, 1))
            weights(Group(0, 1), None)
            groups(sp, GS, body, SPAN)
            for k in range(SPAN - 2, SPAN):
                y_out.wait(sp, Group(GS // SPAN - 1, k, SPAN))

        @block.gpsimd
        def _(pool):
            def gather(g):
                ids_in.wait(pool, g)
                pool.wait_ge(tr_ok.sem, tr_ok.done(g, 2))
                pool.sem_inc(pool_passed, 1)
                for t in range(NU):
                    nc.gpsimd.indirect_dma_start(
                        out=xg[g.u][:, t, :], out_offset=None, in_=dram["x1n"],
                        in_offset=bass.IndirectOffsetOnAxis(ap=ids[g.u][:, t:t + 1], axis=0)).then_inc(xg_in.sems[g.u], 16)

            gather(Group(0, 0, SPAN))
            gather(Group(0, 1, SPAN))

            def body(g):
                if not g.final:
                    gather(g.after_next())

            groups(pool, GS, body, SPAN)

        @block.scalar
        def _(act):
            for c in (xT_ok, even_ok):
                c.start(act)

            def rows(g):
                act.wait_ge(tr_ok.sem, tr_ok.done(g))
                act.wait_ge(mp_ok.sem, mp_ok.done(g, 2))
                for k in range(DK):
                    last = nc.scalar.activation(xT[g.u][:, k, :], tp[k][:, :], ACT.Copy)
                last.then_inc(xT_ok.sem, 1)

            def body(g):
                e = expert(g)
                w_in.wait(act, e)
                act.wait_ge(yp_ok.sem, yp_ok.done(g, 2))
                for f in range(0, FT, 2):
                    act.wait_ge(mp_ok.sem, mp_ok.at(g, f + 1))
                    nc.scalar.activation(mid[g.u][:, f, :], mp[0][:, :], ACT.Relu, bias=b1[e.u][:, f:f + 1])\
                      .then_inc(even_ok.sem, 1)
                if not g.last:
                    rows(g.next())

            rows(Group(0, 0, SPAN))
            groups(act, GS, body, SPAN)

        @block.vector
        def _(dve):
            for c in (odd_ok, y_ok):
                c.start(dve)

            def body(g):
                e = expert(g)
                w_in.wait(dve, e)
                dve.wait_ge(yp_ok.sem, yp_ok.done(g, 2))
                for f in range(1, FT, 2):
                    dve.wait_ge(mp_ok.sem, mp_ok.at(g, f + 1))
                    nc.vector.tensor_scalar(mid[g.u][:, f, :], mp[1][:, :], b1[e.u][:, f:f + 1], 0.0,
                                            ALU.add, ALU.max).then_inc(odd_ok.sem, 1)
                y_out.wait(dve, g, 2)
                b2b = b2[e.u][:, :].rearrange("p (a d) -> p a d", a=1).to_broadcast([P, 2, D])
                for t in range(2):
                    dve.wait_ge(yp_ok.sem, yp_ok.at(g, t + 1))
                    last = nc.vector.tensor_tensor(y[g.u][:, 2 * t:2 * t + 2, :], yp[g.u][t][:, :, :], b2b, ALU.add)
                last.then_inc(y_ok.sem, 1)

            groups(dve, GS, body, SPAN)

        @block.tensor
        def _(pe):
            for c in (tr_ok, mp_ok, yp_ok):
                c.start(pe)
            pe.wait_ge(ident_in, 16)

            def rows(g):
                xg_in.wait(pe, g)
                pe.wait_ge(xT_ok.sem, xT_ok.done(g, 1))
                for k in range(DK):
                    for t in range(NU):
                        last = nc.tensor.transpose(tp[k][:, t * P:(t + 1) * P], xg[g.u][:, t, k * P:(k + 1) * P],
                                                   ident[:, :])
                last.then_inc(tr_ok.sem, 1)

            def body(g):
                e = expert(g)
                w_in.wait(pe, e)
                pe.wait_ge(xT_ok.sem, xT_ok.done(g))
                for f in range(FT):
                    ok = (even_ok, odd_ok)[f % 2]
                    pe.wait_ge(ok.sem, ok.at(g, f // 2))
                    for k in range(DK):
                        last = nc.tensor.matmul(mp[f % 2][:, :], w1[e.u][:, k, f * P:(f + 1) * P], xT[g.u][:, k, :],
                                                start=(k == 0), stop=(k == DK - 1))
                    last.then_inc(mp_ok.sem, 1)
                if not g.last:
                    rows(g.next())
                pe.wait_ge(even_ok.sem, even_ok.done(g))
                pe.wait_ge(odd_ok.sem, odd_ok.done(g))
                pe.wait_ge(y_ok.sem, y_ok.done(g, 2))
                for t in range(NU):
                    for f in range(FT):
                        last = nc.tensor.matmul(yp[g.u][t // 2][:, t % 2, :], mid[g.u][:, f, t * P:(t + 1) * P],
                                                w2[e.u][:, f, :], start=(f == 0), stop=(f == FT - 1))
                    if t % 2:
                        last.then_inc(yp_ok.sem, 1)

            rows(Group(0, 0, SPAN))
            groups(pe, GS, body, SPAN)


def graph_block_1(nc, io, dram, keep):
    with ExitStack() as ctx:
        def sb(name, shape, dt=F32):
            return ctx.enter_context(nc.sbuf_tensor("c_" + name, shape, dt))

        def pb(name, shape, dt=F32):
            return ctx.enter_context(nc.psum_tensor("c_" + name, shape, dt))

        def count(name, n=1):
            return Count(ctx, nc, "c_" + name, n)

        def arrivals(name, n):
            return Arrivals(ctx, nc, "c_" + name, n)

        FT = H1 // P
        w1 = sb("w1", [P, DK, H1])
        w2 = sb("w2", [P, FT, D])
        b1 = sb("b1", [P, FT])
        rw = sb("rw", [P, FT])
        b2 = sb("b2", [P, D])
        eps = sb("eps", [P, 1])
        ident = sb("ident", [P, P])
        eps_eye = sb("eps_eye", [P, P])
        mean1 = sb("mean1", [P, 2])
        ones = sb("ones", [P, P])
        half = sb("half", [P, NU])
        epst = sb("epst", [P, NU])
        ids = [sb(f"ids{u}", [P, NU], U32) for u in range(2)]
        yg = [sb(f"yg{u}", [P, NU, D]) for u in range(2)]
        x1 = [sb(f"x1{u}", [P, NU, D]) for u in range(2)]
        adj = [sb(f"adj{u}", [P, NU, P]) for u in range(2)]
        xb = [sb(f"xb{u}", [P, NU, D]) for u in range(2)]
        xn = [sb(f"xn{u}", [P, NU, D]) for u in range(2)]
        x3 = [sb(f"x3{u}", [P, NU, D]) for u in range(2)]
        up_c = sb("up_c", [P, NU, D])
        dn_c = sb("dn_c", [P, NU, D])
        fin = sb("fin", [P, NU, D])
        hT = [sb(f"hT{u}", [P, DK, W]) for u in range(2)]
        hid = [sb(f"hid{u}", [P, FT, W]) for u in range(2)]
        sq = [sb(f"sq{u}", [P, W]) for u in range(2)]
        sqs = sb("sqs", [P, W])
        ms = sb("ms", [P, NU])
        rr = sb("rr", [P, NU])
        diag = sb("diag", [P, W])
        stats = sb("stats", [P, NU, 6])
        mv = sb("mv", [P, NU, 2])
        rs = sb("rs", [P, NU])
        hp = [pb(f"hp{k}", [P, W]) for k in range(DK)]
        mp = [pb(f"mp{k}", [P, W]) for k in range(2)]
        yp = [pb(f"yp{k}", [P, 2, D]) for k in range(2)]
        msp = pb("msp", [P, NU, 2])
        rrp = pb("rrp", [P, W])

        consts = ctx.enter_context(nc.semaphore("c_consts"))
        setup = ctx.enter_context(nc.semaphore("c_setup"))
        passed = ctx.enter_context(nc.semaphore("c_passed"))
        pool_passed = ctx.enter_context(nc.semaphore("c_pool_passed"))
        x1_in = arrivals("x1_in", 16)
        adj_in = arrivals("adj_in", 16)
        yg_in = arrivals("yg_in", 16 * NU)
        x3_out = arrivals("x3_out", 16)
        ids_ok = count("ids_ok")
        gd_ok = count("gd_ok", 4)
        gdx_ok = count("gdx_ok")
        st_ok = count("st_ok")
        mv_ok = count("mv_ok")
        var_ok = count("var_ok")
        rs_ok = count("rs_ok")
        xn_ok = count("xn_ok")
        adj_ok = count("adj_ok")
        xb_ok = count("xb_ok")
        hp_ok = count("hp_ok")
        hT_ok = count("hT_ok")
        mp_ok = count("mp_ok", FT)
        hid_ok = count("hid_ok", FT)
        sqs_ok = count("sqs_ok", FT)
        msp_ok = count("msp_ok")
        dg_ok = count("dg_ok")
        rrp_ok = count("rrp_ok")
        ms_ok = count("ms_ok")
        rr_ok = count("rr_ok")
        hn_ok = count("hn_ok", FT)
        act_ok = count("act_ok", FT)
        yp_ok = count("yp_ok", 2)
        x3_ok = count("x3_ok")
        block = ctx.enter_context(nc.Block())

        x1v, av, x3v = by_tokens(dram["x1"]), by_tokens(io["adjT"]), by_tokens(dram["x3"])
        N_CONST = 7

        def cols(g):
            return slice(g.n * NU, g.n * NU + NU) if isinstance(g.n, int) else bass.ds(g.n * NU, NU)

        @block.sync
        def _(sp):
            for dst, src in ((w1[:, :, :], io["W1c"].rearrange("(k p) f -> p k f", p=P)),
                             (w2[:, :, :], io["W2c"].rearrange("(k p) f -> p k f", p=P)),
                             (b1[:, :], io["b1c"]), (rw[:, :], io["rms_w"]), (b2[:, :], io["b2c"]),
                             (eps[:, :], io["eps1"]), (ident[:, :], io["ident"])):
                sp.dma_start(dst, src).then_inc(consts, 16)

            def load(g):
                sp.wait_ge(xb_ok.sem, xb_ok.done(g, 2))
                sp.dma_start(x1[g.u][:, :, :], g.of(x1v)).then_inc(x1_in.sems[g.u], 16)
                sp.wait_ge(hp_ok.sem, hp_ok.done(g, 2))
                sp.dma_start(adj[g.u][:, :, :], g.of(av)).then_inc(adj_in.sems[g.u], 16)

            def body(g):
                if not g.final:
                    load(g.after_next())
                sp.wait_ge(x3_ok.sem, x3_ok.done(g))
                sp.dma_start(g.of(x3v), x3[g.u][:, :, :]).then_inc(x3_out.sems[g.u], 16)

            load(Group(0, 0))
            load(Group(0, 1))
            groups(sp, G, body)
            for u in range(2):
                x3_out.wait(sp, Group(G // 2 - 1, u))

        @block.gpsimd
        def _(pool):
            for c in (ids_ok, var_ok, rs_ok, xb_ok, rr_ok):
                c.start(pool)
            pool.wait_ge(setup, 7)

            def gather(g):
                pool.wait_ge(gd_ok.sem, gd_ok.done(g, 2))
                yg_in.wait(pool, g, 2)
                pool.sem_inc(pool_passed, 1)
                nc.gpsimd.tensor_copy(ids[g.u][:, :], keep["slot"][:, cols(g)]).then_inc(ids_ok.sem, 1)
                pool.wait_ge(ids_ok.sem, ids_ok.done(g))
                pool.sem_inc(pool_passed, 1)
                for t in range(NU):
                    nc.gpsimd.indirect_dma_start(
                        out=yg[g.u][:, t, :], out_offset=None, in_=dram["y"],
                        in_offset=bass.IndirectOffsetOnAxis(ap=ids[g.u][:, t:t + 1], axis=0))\
                        .then_inc(yg_in.sems[g.u], 16)

            def inverse_root(g):
                pool.wait_ge(mv_ok.sem, mv_ok.done(g))
                pool.wait_ge(xn_ok.sem, xn_ok.done(g, 1))
                nc.gpsimd.tensor_tensor(rs[:, :], mv[:, :, 1], epst[:, :], ALU.add).then_inc(var_ok.sem, 1)
                pool.wait_ge(var_ok.sem, var_ok.done(g))
                nc.gpsimd.tensor_tensor(rs[:, :], rs[:, :], half[:, :], ALU.pow).then_inc(rs_ok.sem, 1)

            def bias(g):
                pool.wait_ge(x3_ok.sem, x3_ok.done(g, 2))
                pool.wait_ge(xn_ok.sem, xn_ok.done(g))
                nc.gpsimd.tensor_tensor(xb[g.u][:, :, :], x1[g.u][:, :, :],
                                        b2[:, :].rearrange("p (a d) -> p a d", a=1).to_broadcast([P, NU, D]),
                                        ALU.add).then_inc(xb_ok.sem, 1)

            def root_of_squares(g):
                pool.wait_ge(ms_ok.sem, ms_ok.done(g))
                pool.wait_ge(dg_ok.sem, dg_ok.done(g, 1))
                nc.gpsimd.tensor_tensor(rr[:, :], ms[:, :], half[:, :], ALU.pow).then_inc(rr_ok.sem, 1)

            def body(g):
                if not g.final:
                    gather(g.after_next())
                if not g.last:
                    root_of_squares(g.next())
                if not g.final:
                    inverse_root(g.after_next())
                    bias(g.after_next())

            for u in range(2):
                gather(Group(0, u))
            for u in range(2):
                inverse_root(Group(0, u))
                bias(Group(0, u))
            root_of_squares(Group(0, 0))
            groups(pool, G, body)

        @block.vector
        def _(dve):
            for c in (gd_ok, gdx_ok, st_ok, mv_ok, xn_ok, adj_ok, sqs_ok, ms_ok, dg_ok, hn_ok, x3_ok):
                c.start(dve)
            dve.wait_ge(consts, 16 * N_CONST)
            nc.vector.memset(half[:, :], -0.5).then_inc(setup, 1)
            nc.vector.memset(epst[:, :], LN_EPS).then_inc(setup, 1)
            nc.vector.memset(mean1[:, :], 1.0 / H1).then_inc(setup, 1)
            nc.vector.memset(ones[:, :], 1.0).then_inc(setup, 1)
            nc.vector.tensor_scalar(eps_eye[:, :], ident[:, :], eps[:, :], None, ALU.mult).then_inc(setup, 3)
            dve.wait_ge(setup, 7)

            def prepare(g, guarded):
                if not guarded:
                    x1_in.wait(dve, g)
                    yg_in.wait(dve, g)
                    gate = keep["gate"][:, cols(g)].rearrange("p (u a) -> p u a", a=1).to_broadcast([P, NU, D])
                    nc.vector.tensor_tensor(yg[g.u][:, :, :], yg[g.u][:, :, :], gate, ALU.mult).then_inc(gd_ok.sem, 1)
                    return
                dve.wait_ge(gd_ok.sem, gd_ok.at(g, 1))
                nc.vector.tensor_scalar(up_c[:, :, :], yg[g.u][:, :, :], 0.0, CLAMP, ALU.max, ALU.min)
                nc.vector.tensor_scalar(dn_c[:, :, :], yg[g.u][:, :, :], 0.0, -CLAMP, ALU.min, ALU.max)
                nc.vector.tensor_scalar(fin[:, :, :], yg[g.u][:, :, :], 0.0, 0.0, ALU.mult, ALU.is_equal)\
                  .then_inc(gd_ok.sem, 1)
                dve.wait_ge(gd_ok.sem, gd_ok.at(g, 2))
                nc.vector.tensor_tensor(up_c[:, :, :], up_c[:, :, :], dn_c[:, :, :], ALU.add).then_inc(gd_ok.sem, 1)
                dve.wait_ge(gd_ok.sem, gd_ok.at(g, 3))
                dve.sem_inc(passed, 1)
                nc.vector.copy_predicated(up_c[:, :, :], fin[:, :, :].bitcast(U32), yg[g.u][:, :, :])\
                  .then_inc(gd_ok.sem, 1)
                dve.wait_ge(gd_ok.sem, gd_ok.at(g, 4))
                nc.vector.tensor_tensor(x1[g.u][:, :, :], x1[g.u][:, :, :], up_c[:, :, :], ALU.add)\
                  .then_inc(gdx_ok.sem, 1)
                dve.wait_ge(gdx_ok.sem, gdx_ok.done(g))
                for t in range(NU):
                    last = nc.vector.bn_stats(stats[:, t, :], x1[g.u][:, t, :])
                last.then_inc(st_ok.sem, 1)
                adj_in.wait(dve, g)
                nc.vector.tensor_tensor(adj[g.u][:, :, :], adj[g.u][:, :, :],
                                        eps_eye[:, :].rearrange("p (a q) -> p a q", a=1).to_broadcast([P, NU, P]),
                                        ALU.add).then_inc(adj_ok.sem, 1)
                dve.wait_ge(st_ok.sem, st_ok.done(g))
                dve.sem_inc(passed, 1)
                for t in range(NU):
                    last = nc.vector.bn_aggr(mv[:, t, :], stats[:, t, :])
                last.then_inc(mv_ok.sem, 1)

            def normalise(g):
                dve.wait_ge(rs_ok.sem, rs_ok.done(g))
                dve.wait_ge(hp_ok.sem, hp_ok.done(g, 2))
                for t in range(NU):
                    last = nc.vector.tensor_scalar(xn[g.u][:, t, :], x1[g.u][:, t, :], mv[:, t, 0:1], rs[:, t:t + 1],
                                                   ALU.subtract, ALU.mult)
                last.then_inc(xn_ok.sem, 1)

            def squares(g):
                for f in range(FT):
                    dve.wait_ge(hid_ok.sem, hid_ok.at(g, f + 1))
                    if f == 0:
                        dve.wait_ge(msp_ok.sem, msp_ok.done(g, 1))
                        nc.vector.tensor_copy(sqs[:, :], sq[0][:, :]).then_inc(sqs_ok.sem, 1)
                    else:
                        dve.wait_ge(sqs_ok.sem, sqs_ok.at(g, f))
                        nc.vector.tensor_tensor(sqs[:, :], sqs[:, :], sq[f % 2][:, :], ALU.add).then_inc(sqs_ok.sem, 1)

            def mean_square(g):
                dve.wait_ge(msp_ok.sem, msp_ok.done(g))
                dve.wait_ge(rr_ok.sem, rr_ok.done(g, 1))
                nc.vector.tensor_scalar(ms[:, :], msp[:, :, 0], RMS_EPS, None, ALU.add).then_inc(ms_ok.sem, 1)

            def diagonal(g):
                dve.wait_ge(rr_ok.sem, rr_ok.done(g))
                dve.wait_ge(rrp_ok.sem, rrp_ok.done(g, 1))
                for t in range(NU):
                    last = nc.vector.tensor_scalar(diag[:, t * P:(t + 1) * P], ident[:, :], rr[:, t:t + 1], None, ALU.mult)
                last.then_inc(dg_ok.sem, 1)

            def rms(g):
                dve.wait_ge(rrp_ok.sem, rrp_ok.done(g))
                for f in range(FT):
                    nc.vector.scalar_tensor_tensor(hid[g.u][:, f, :], hid[g.u][:, f, :], rw[:, f:f + 1], rrp[:, :],
                                                   ALU.mult, ALU.mult).then_inc(hn_ok.sem, 1)

            def body(g):
                if not g.last:
                    squares(g.next())
                if not g.last:
                    mean_square(g.next())
                if not g.final:
                    prepare(g.after_next(), False)
                if not g.last:
                    diagonal(g.next())
                if not g.final:
                    prepare(g.after_next(), True)
                    normalise(g.after_next())
                if not g.last:
                    rms(g.next())
                dve.wait_ge(xb_ok.sem, xb_ok.done(g))
                x3_out.wait(dve, g, 2)
                for t in range(2):
                    dve.wait_ge(yp_ok.sem, yp_ok.at(g, t + 1))
                    last = nc.vector.tensor_tensor(x3[g.u][:, 2 * t:2 * t + 2, :], yp[t][:, :, :],
                                                   xb[g.u][:, 2 * t:2 * t + 2, :], ALU.add)
                last.then_inc(x3_ok.sem, 1)

            for u in range(2):
                prepare(Group(0, u), False)
                prepare(Group(0, u), True)
                normalise(Group(0, u))
            squares(Group(0, 0))
            mean_square(Group(0, 0))
            diagonal(Group(0, 0))
            rms(Group(0, 0))
            groups(dve, G, body)

        @block.scalar
        def _(act):
            for c in (hT_ok, hid_ok, act_ok):
                c.start(act)
            act.wait_ge(setup, 7)

            def up(g):
                act.wait_ge(hp_ok.sem, hp_ok.done(g))
                act.wait_ge(mp_ok.sem, mp_ok.done(g, 2))
                for k in range(DK):
                    last = nc.scalar.activation(hT[g.u][:, k, :], hp[k][:, :], ACT.Copy)
                last.then_inc(hT_ok.sem, 1)
                act.wait_ge(yp_ok.sem, yp_ok.done(g, 2))
                for f in range(FT):
                    act.wait_ge(mp_ok.sem, mp_ok.at(g, f + 1))
                    nc.scalar.activation(hid[g.u][:, f, :], mp[f % 2][:, :], ACT.Identity, bias=b1[:, f:f + 1])
                    act.wait_ge(sqs_ok.sem, sqs_ok.at(g, f - 1))
                    nc.scalar.activation(sq[f % 2][:, :], mp[f % 2][:, :], ACT.Square, bias=b1[:, f:f + 1])\
                      .then_inc(hid_ok.sem, 1)

            def silu(g):
                for f in range(FT):
                    act.wait_ge(hn_ok.sem, hn_ok.at(g, f + 1))
                    nc.scalar.activation(hid[g.u][:, f, :], hid[g.u][:, f, :], ACT.Silu).then_inc(act_ok.sem, 1)

            def body(g):
                if not g.last:
                    up(g.next())
                    silu(g.next())

            up(Group(0, 0))
            silu(Group(0, 0))
            groups(act, G, body)

        @block.tensor
        def _(pe):
            for c in (hp_ok, mp_ok, msp_ok, rrp_ok, yp_ok):
                c.start(pe)
            pe.wait_ge(setup, 7)

            def up(g):
                pe.wait_ge(xn_ok.sem, xn_ok.done(g))
                pe.wait_ge(adj_ok.sem, adj_ok.done(g))
                pe.wait_ge(hT_ok.sem, hT_ok.done(g, 1))
                for k in range(DK):
                    for t in range(NU):
                        last = nc.tensor.matmul(hp[k][:, t * P:(t + 1) * P], xn[g.u][:, t, k * P:(k + 1) * P],
                                                adj[g.u][:, t, :], start=True, stop=True)
                last.then_inc(hp_ok.sem, 1)
                pe.wait_ge(hT_ok.sem, hT_ok.done(g))
                for f in range(FT):
                    pe.wait_ge(hid_ok.sem, hid_ok.at(g, f - 1))
                    for k in range(DK):
                        last = nc.tensor.matmul(mp[f % 2][:, :], w1[:, k, f * P:(f + 1) * P], hT[g.u][:, k, :],
                                                start=(k == 0), stop=(k == DK - 1))
                    last.then_inc(mp_ok.sem, 1)

            def square_sum(g):
                pe.wait_ge(sqs_ok.sem, sqs_ok.done(g))
                pe.wait_ge(ms_ok.sem, ms_ok.done(g, 1))
                for t in range(NU):
                    last = nc.tensor.matmul(msp[:, t, :], sqs[:, t * P:(t + 1) * P], mean1[:, :], start=True, stop=True)
                last.then_inc(msp_ok.sem, 1)

            def spread(g):
                pe.wait_ge(dg_ok.sem, dg_ok.done(g))
                pe.wait_ge(hn_ok.sem, hn_ok.done(g, 1))
                nc.tensor.matmul(rrp[:, :], ones[:, :], diag[:, :], start=True, stop=True).then_inc(rrp_ok.sem, 1)

            def down(g, tiles):
                for t in tiles:
                    for f in range(FT):
                        last = nc.tensor.matmul(yp[t // 2][:, t % 2, :], hid[g.u][:, f, t * P:(t + 1) * P],
                                                w2[:, f, :], start=(f == 0), stop=(f == FT - 1))
                last.then_inc(yp_ok.sem, 1)

            def body(g):
                if not g.last:
                    up(g.next())
                    square_sum(g.next())
                pe.wait_ge(act_ok.sem, act_ok.done(g))
                pe.wait_ge(x3_ok.sem, x3_ok.done(g, 1))
                down(g, (0, 1))
                if not g.last:
                    spread(g.next())
                down(g, (2, 3))

            up(Group(0, 0))
            square_sum(Group(0, 0))
            spread(Group(0, 0))
            groups(pe, G, body)


def attention(nc, io, dram, out):
    with ExitStack() as ctx:
        def sb(name, shape, dt=F32):
            return ctx.enter_context(nc.sbuf_tensor("d_" + name, shape, dt))

        def pb(name, shape, dt=F32):
            return ctx.enter_context(nc.psum_tensor("d_" + name, shape, dt))

        def count(name, n=1):
            return Count(ctx, nc, "d_" + name, n)

        def arrivals(name, n):
            return Arrivals(ctx, nc, "d_" + name, n)

        CP = C1 // 2
        NS = NU * CH
        R = P // E1

        ident = sb("ident", [P, P])
        nw = sb("nw", [P, D])
        rw = sb("rw", [P, CP, E1])
        rb = sb("rb", [P, E1])
        wq = sb("wq", [DH, EH, P])
        wk = sb("wk", [DH, EH, P])
        A = sb("A", [P, EH, P])
        At = sb("At", [P, EH, P], F32R)
        wv = sb("wv", [P, 2, E1 * DC])
        wp = sb("wp", [P, NH, DC])
        pb2 = sb("pb2", [P, E1])
        pbx = sb("pbx", [P, P])
        owT = sb("owT", [P, CP, D])
        pbo = sb("pbo", [P, D])
        pick_f = sb("pick_f", [P, CH, P])
        pick = sb("pick", [P, CH, P], F32R)
        ones = sb("ones", [P, R])
        half = sb("half", [P, NU])
        epst = sb("epst", [P, NU])

        x = [sb(f"x{u}", [P, NU, D]) for u in range(2)]
        xin = sb("xin", [P, NU, D])
        xn = sb("xn", [P, NU, D])
        stats = sb("stats", [P, NU, 6])
        mv = sb("mv", [P, NU, 2])
        rs = [sb(f"rs{k}", [P, NU]) for k in range(2)]
        vv = sb("vv", [P, NU])
        xT = sb("xT", [P, CP, W])
        xTr = sb("xTr", [P, CP, W], F32R)
        xp = [sb(f"xp{u}", [P, C1, W]) for u in range(2)]
        xpr = [sb(f"xpr{u}", [P, C1, W], F32R) for u in range(1)]
        up = sb("up", [P, CP, NH, NU, E1, P], F32R)
        uf = sb("uf", [P, CP, NH, NU, E1, P])
        v = sb("v", [P, NU, CP, 2, E1, NH, DH])
        mx = [sb(f"mx{k}", [P, P]) for k in range(2)]
        mxT = [sb(f"mxT{k}", [P, P], F32R) for k in range(2)]
        mrow = sb("mrow", [P, NU, E1 * P], F32R)
        lg = sb("lg", [P, NU, E1])
        lm = sb("lm", [P, NU])
        ex = sb("ex", [P, NU, E1])
        es = sb("es", [P, NU])
        gate = sb("gate", [P, NU, E1])
        gate_r = sb("gate_r", [P, NU, E1, R])
        gateT = sb("gateT", [P, NU, P])
        pt = [sb(f"pt{k}", [P, E1, P]) for k in range(4)]
        rec2 = [sb(f"rec{k}", [P, NH, P]) for k in range(2)]
        yn = [sb(f"yn{k}", [P, C1, NH, P]) for k in range(2)]
        oT = [sb(f"oT{k}", [P, CP, P]) for k in range(2)]
        res = [sb(f"res{u}", [P, NU, D]) for u in range(2)]

        gen = [pb(f"gen{k}", [P, W]) for k in range(2)]
        sn = [pb(f"sn{k}", [P, W]) for k in range(2)]
        st = [pb(f"st{k}", [P, W]) for k in range(2)]
        av = [pb(f"av{k}", [P, 2, NH, P]) for k in range(2)]

        fills = [("u", cp, h, e) for cp in range(CP) for h in range(NH) for e in range(E1)]
        fills += [("v", b, cp) for b in range(NU) for cp in range(CP)]
        first = [("rows", cp) for cp in range(CP)]
        first += [("up", cp, h, e) for cp in range(CP) for h in range(NH) for e in range(E1)] + [("router",)]
        middle, left = [], list(fills)
        for k in range(NS):
            middle.append((None, k))
            if k % 4 != 3:
                middle.append(left.pop(0))
            if k == 21:
                middle.append(("max", 0))
        middle += left + [("gates",), ("max", 1)]
        steps = []
        for k in range(NS + 10):
            if k < NS:
                steps.append(("s", k))
            if 2 <= k < NS + 2:
                steps.append(("a", k - 2))
            if k >= 12 and (k - 12) % CH == 0:
                steps.append(("proj", (k - 12) // CH))
            if k >= 15 and (k - 15) % CH == 0:
                steps.append(("fin", (k - 15) // CH))
        for b in range(NU):
            for w in ("proj", "fin"):
                if (w, b) not in steps:
                    steps.append((w, b))
        uses = first + [m for m in middle if m[0] is not None] + [m for m in steps if m[0] in ("proj", "fin")]
        turn = {use: (k % 2, k // 2) for k, use in enumerate(uses)}
        assert len(uses) % 2 == 0 and len(turn) == len(uses)

        consts = ctx.enter_context(nc.semaphore("d_consts"))
        wv_in = ctx.enter_context(nc.semaphore("d_wv_in"))
        sp_passed = ctx.enter_context(nc.semaphore("d_sp_passed"))
        zeroed = ctx.enter_context(nc.semaphore("d_zeroed"))
        products = ctx.enter_context(nc.semaphore("d_products"))
        setup = ctx.enter_context(nc.semaphore("d_setup"))
        passed = ctx.enter_context(nc.semaphore("d_passed"))
        pool_passed = ctx.enter_context(nc.semaphore("d_pool_passed"))
        gen_ok = [count(f"gen_ok{k}", len(uses) // 2) for k in range(2)]
        gen_out = [count(f"gen_out{k}", len(uses) // 2) for k in range(2)]
        x_in = arrivals("x_in", 16)
        o_out = arrivals("o_out", 16)
        row_in = [ctx.enter_context(nc.semaphore(f"d_row_in{k}")) for k in range(2)]
        st_ok = count("st_ok")
        mv_ok = count("mv_ok")
        rs_ok = count("rs_ok", 6)
        xin_ok = count("xin_ok")
        xn_ok = count("xn_ok")
        res_ok = count("res_ok")
        tr_ok = count("tr_ok")
        xTr_ok = count("xTr_ok")
        xpr_ok = count("xpr_ok")
        xp_ok = count("xp_ok")
        sn_ok = count("sn_ok", NS)
        mx_ok = count("mx_ok", NS)
        lg_ok = count("lg_ok", 3)
        ex_ok = count("ex_ok")
        ga_ok = count("ga_ok", 4)
        s_ok = count("s_ok", NS)
        e_ok = count("e_ok", NS)
        a_ok = count("a_ok", NS)
        rc_ok = count("rc_ok", NS)
        yn_ok = count("yn_ok", NS // 2)
        o_ok = count("o_ok")
        block = ctx.enter_context(nc.Block())

        xv, ov = by_tokens(dram["x3"]), by_tokens(out)
        N_CONST = 10
        SETUP = 19

        def tile_view(t):
            return t[:, :] if len(t.shape) == 2 else t[:, :, :]

        def written(eng, use, g):
            bank, pos = turn[use]
            eng.wait_ge(gen_ok[bank].sem, gen_ok[bank].at(g, pos + 1))
            return gen[bank]

        def read(ins, use):
            ins.then_inc(gen_out[turn[use][0]].sem, 1)

        def was_read(eng, use, g):
            bank, pos = turn[use]
            eng.wait_ge(gen_out[bank].sem, gen_out[bank].at(g, pos + 1))

        @block.sync
        def _(sp):
            for dst, src in ((ident[:, :], io["ident"]), (nw[:, :], io["norm_w"]),
                             (rw[:, :, :], io["router_w"].rearrange("(k p) e -> p k e", p=P)),
                             (rb[:, :], io["router_b"]),
                             (wq[:, :, :], io["wq"].rearrange("p (k i) -> p k i", k=EH)),
                             (wk[:, :, :], io["wk"].rearrange("p (k i) -> p k i", k=EH)),
                             (wp[:, :, :], io["wp"].rearrange("p (h o) -> p h o", h=NH)),
                             (pb2[:, :], io["pb"]),
                             (owT[:, :, :], io["owT"].rearrange("(k p) n -> p k n", p=P)),
                             (pick_f[:, :, :], io["pick"].rearrange("p (c q) -> p c q", c=CH))):
                sp.dma_start(dst, src).then_inc(consts, 16)
            sp.wait_ge(zeroed, 1)
            for k in range(2):
                sp.dma_start(wv[DC * k:DC * (k + 1), k, :], io["wv"]).then_inc(wv_in, 16)

            def load(g):
                sp.wait_ge(res_ok.sem, res_ok.done(g, 2))
                sp.dma_start(x[g.u][:, :, :], g.of(xv)).then_inc(x_in.sems[g.u], 16)

            load(Group(0, 0))
            load(Group(0, 1))

            def body(g):
                for half_ in range(2):
                    was_read(sp, ("max", half_), g)
                    sp.sem_inc(sp_passed, 1)
                    sp.wait_ge(s_ok.sem, s_ok.done(g, 1))
                    for b in range(2):
                        sp.dma_start(mrow[0:CH, 2 * half_ + b, :].bitcast(F32),
                                     mxT[half_][32 * b:32 * b + 32, :].bitcast(F32))\
                            .then_inc(row_in[half_], 16)
                if not g.final:
                    load(g.after_next())
                sp.wait_ge(o_ok.sem, o_ok.done(g))
                sp.dma_start(g.of(ov), res[g.u][:, :, :]).then_inc(o_out.sems[g.u], 16)

            groups(sp, G, body)
            for u in range(2):
                o_out.wait(sp, Group(G // 2 - 1, u))

        @block.gpsimd
        def _(pool):
            for c in (rs_ok, res_ok):
                c.start(pool)
            nc.gpsimd.memset(wv[:, :, :], 0.0).then_inc(zeroed, 1)
            for u in range(2):
                nc.gpsimd.memset(xp[u][:, :, :], 0.0).then_inc(setup, 1)
            pool.wait_ge(setup, SETUP)

            def inverse_roots(g):
                a, b = rs
                steps_ = ((a, mv[:, :, 1], epst, ALU.add), (a, a, half, ALU.pow), (vv, a, a, ALU.mult),
                          (vv, vv, mv[:, :, 1], ALU.mult), (vv, vv, epst, ALU.add), (b, vv, half, ALU.pow))
                pool.wait_ge(mv_ok.sem, mv_ok.done(g))
                pool.wait_ge(xn_ok.sem, xn_ok.done(g, 1))
                for n, (dst, p, q, op) in enumerate(steps_):
                    if n:
                        pool.wait_ge(rs_ok.sem, rs_ok.at(g, n))
                    nc.gpsimd.tensor_tensor(dst[:, :], p if n in (0,) else p[:, :],
                                            q if n == 3 else q[:, :], op).then_inc(rs_ok.sem, 1)

            def residual(g):
                pool.wait_ge(xin_ok.sem, xin_ok.done(g))
                o_out.wait(pool, g, 2)
                nc.gpsimd.tensor_tensor(res[g.u][:, :, :], x[g.u][:, :, :], xin[:, :, :], ALU.add)\
                  .then_inc(res_ok.sem, 1)

            def body(g):
                if not g.last:
                    inverse_roots(g.next())
                    residual(g.next())

            inverse_roots(Group(0, 0))
            residual(Group(0, 0))
            groups(pool, G, body)

        @block.vector
        def _(dve):
            for c in (st_ok, mv_ok, xin_ok, xn_ok, xTr_ok, xpr_ok, xp_ok, mx_ok, lg_ok, ga_ok, rc_ok, yn_ok, o_ok):
                c.start(dve)
            for tile, value in ((A, 0.0), (pbx, 0.0), (ones, 1.0), (half, -0.5), (epst, LN_EPS), (mx[0], 0.0),
                                (mx[1], 0.0)):
                nc.vector.memset(tile_view(tile), value).then_inc(setup, 1)
            for tile in (At, xpr[0], mrow):
                nc.vector.memset(tile_view(tile).bitcast(F32), 0.0).then_inc(setup, 1)
            dve.wait_ge(consts, 16 * N_CONST)
            dve.wait_ge(setup, 12)
            nc.vector.tensor_copy(pick[:, :, :], pick_f[:, :, :]).then_inc(setup, 1)
            nc.vector.tensor_copy(pbx[:, :].rearrange("p (e r) -> p e r", e=E1)[:, :, 0], pb2[:, :])\
              .then_inc(setup, 1)
            dve.wait_ge(products, 1)
            for k in range(2):
                r = slice(DC * k, DC * k + DC)
                nc.vector.tensor_copy(A[r, :, r], sn[0][r, :].rearrange("p (j i) -> p j i", j=EH)).then_inc(setup, 1)
                nc.vector.tensor_copy(At[r, :, r], sn[1][r, :].rearrange("p (j i) -> p j i", j=EH)).then_inc(setup, 1)
            dve.wait_ge(products, 2)
            nc.vector.tensor_copy(pbo[:, :], st[0][:, 0:D]).then_inc(setup, 1)
            dve.wait_ge(setup, SETUP)

            def statistics(g):
                x_in.wait(dve, g)
                for t in range(NU):
                    last = nc.vector.bn_stats(stats[:, t, :], x[g.u][:, t, :])
                last.then_inc(st_ok.sem, 1)
                dve.wait_ge(st_ok.sem, st_ok.done(g))
                dve.wait_ge(rs_ok.sem, rs_ok.done(g, 1))
                dve.sem_inc(passed, 1)
                for t in range(NU):
                    last = nc.vector.bn_aggr(mv[:, t, :], stats[:, t, :])
                last.then_inc(mv_ok.sem, 1)

            def normalise(g):
                dve.wait_ge(rs_ok.sem, rs_ok.done(g))
                dve.wait_ge(res_ok.sem, res_ok.done(g, 1))
                for t in range(NU):
                    last = nc.vector.tensor_scalar(xin[:, t, :], x[g.u][:, t, :], mv[:, t, 0:1], rs[0][:, t:t + 1],
                                                   ALU.subtract, ALU.mult)
                last.then_inc(xin_ok.sem, 1)

            def normalise_again(g):
                dve.wait_ge(xin_ok.sem, xin_ok.done(g))
                dve.wait_ge(tr_ok.sem, tr_ok.done(g, 1))
                for t in range(NU):
                    last = nc.vector.scalar_tensor_tensor(xn[:, t, :], xin[:, t, :], rs[1][:, t:t + 1], nw[:, :],
                                                          ALU.mult, ALU.mult)
                last.then_inc(xn_ok.sem, 1)

            def spread(tile, shape):
                return tile.rearrange("p (u a) -> p u a", a=1).to_broadcast(shape)

            def gates(g):
                bank = written(dve, ("router",), g)
                nc_ = nc.vector.tensor_tensor(lg[:, :, :], bank[:, 0:NU * E1].rearrange("p (u e) -> p u e", u=NU),
                                              rb[:, :].rearrange("p (a e) -> p a e", a=1).to_broadcast([P, NU, E1]),
                                              ALU.add)
                read(nc_, ("router",))
                was_read(dve, ("router",), g)
                nc.vector.tensor_reduce(lm[:, :], lg[:, :, :], AX.X, ALU.max).then_inc(lg_ok.sem, 1)
                dve.wait_ge(lg_ok.sem, lg_ok.at(g, 1))
                nc.vector.tensor_tensor(lg[:, :, :], lg[:, :, :], spread(lm[:, :], [P, NU, E1]), ALU.subtract)\
                  .then_inc(lg_ok.sem, 2)

            def gates_on(g):
                dve.wait_ge(ex_ok.sem, ex_ok.done(g))
                nc.vector.tensor_reduce(es[:, :], ex[:, :, :], AX.X, ALU.add).then_inc(ga_ok.sem, 1)
                dve.wait_ge(ga_ok.sem, ga_ok.at(g, 1))
                nc.vector.reciprocal(es[:, :], es[:, :]).then_inc(ga_ok.sem, 1)
                dve.wait_ge(ga_ok.sem, ga_ok.at(g, 2))
                nc.vector.tensor_tensor(gate[:, :, :], ex[:, :, :], spread(es[:, :], [P, NU, E1]), ALU.mult)\
                  .then_inc(ga_ok.sem, 1)
                dve.wait_ge(ga_ok.sem, ga_ok.at(g, 3))
                nc.vector.tensor_copy(gate_r[:, :, :, :].rearrange("p u e r -> p (u e) r"),
                                      gate[:, :, :].rearrange("p u (e a) -> p (u e) a", a=1)
                                      .to_broadcast([P, NU * E1, R])).then_inc(ga_ok.sem, 1)

            def chunk_copies(g):
                was_read(dve, ("rows", 1), g)
                dve.wait_ge(sn_ok.sem, sn_ok.done(g, 1))
                nc.vector.tensor_copy(xTr[:, :, :], xT[:, :, :]).then_inc(xTr_ok.sem, 1)
                for c in range(C1):
                    r = slice(DC * (c % 2), DC * (c % 2) + DC)
                    last = nc.vector.tensor_copy(xpr[0][r, c, :], xT[r, c // 2, :])
                last.then_inc(xpr_ok.sem, 1)
                dve.wait_ge(s_ok.sem, s_ok.done(g, 2))
                for c in range(C1):
                    r = slice(DC * (c % 2), DC * (c % 2) + DC)
                    last = nc.vector.tensor_copy(xp[g.u][r, c, :], xT[r, c // 2, :])
                last.then_inc(xp_ok.sem, 1)

            def body(g):
                chunk_copies(g)
                gates(g)
                for m in middle:
                    if m[0] is None:
                        k = m[1]
                        b, ch = k // CH, k % CH
                        dve.wait_ge(sn_ok.sem, sn_ok.at(g, k + 1))
                        nc.vector.tensor_reduce(mx[b // 2][:, 32 * (b % 2) + E1 * ch:32 * (b % 2) + E1 * (ch + 1)],
                                                sn[k % 2][:, :].rearrange("p (e s) -> p e s", e=E1), AX.X, ALU.max,
                                                negate=True).then_inc(mx_ok.sem, 1)
                        if k == 3:
                            gates_on(g)
                    elif m[0] == "max":
                        bank = written(dve, m, g)
                        dve.wait_ge(row_in[m[1]], rows_before(g))
                        read(nc.vector.tensor_copy(mxT[m[1]][:, :], bank[:, 0:P]), m)
                for what, k in steps:
                    if what == "a" and k % 2:
                        j = k // 2
                        b, c = j // C1, j % C1
                        bank, rec = av[j % 2], rec2[j % 2]
                        dve.wait_ge(a_ok.sem, a_ok.at(g, k + 1))
                        nc.vector.reciprocal(rec[:, :, :], bank[:, 1, :, :]).then_inc(rc_ok.sem, 1)
                        dve.wait_ge(rc_ok.sem, rc_ok.at(g, 2 * j + 1))
                        if j == 0:
                            was_read(dve, ("gates",), g)
                        nc.vector.tensor_tensor(rec[:, :, :], rec[:, :, :],
                                                gateT[:, b, :].rearrange("p (a t) -> p a t", a=1).to_broadcast([P, NH, P]),
                                                ALU.mult).then_inc(rc_ok.sem, 1)
                        dve.wait_ge(rc_ok.sem, rc_ok.at(g, 2 * j + 2))
                        if c == 0:
                            if b >= 2:
                                was_read(dve, ("proj", b - 2), g)
                            else:
                                proj_before(dve, b + 2, g)
                        nc.vector.tensor_tensor(yn[b % 2][:, c, :, :], bank[:, 0, :, :], rec[:, :, :], ALU.mult)\
                          .then_inc(yn_ok.sem, 1)
                        if not g.last:
                            if j == 3:
                                statistics(g.next())
                            if j == 6:
                                normalise(g.next())
                            if j == 9:
                                normalise_again(g.next())
                    elif what == "fin":
                        bank = written(dve, (what, k), g)
                        if k == 0:
                            dve.wait_ge(res_ok.sem, res_ok.done(g))
                        ins = nc.vector.tensor_tensor(res[g.u][:, k, :], bank[:, 0:D], res[g.u][:, k, :], ALU.add)
                        read(ins, (what, k))
                was_read(dve, ("fin", NU - 1), g)
                dve.sem_inc(o_ok.sem, 1)

            def rows_before(g):
                return g.n * 32

            def proj_before(eng, b, g):
                bank, pos = turn[("proj", b)]
                eng.wait_ge(gen_out[bank].sem, gen_out[bank].at(g, pos + 1) - gen_out[bank].n)

            statistics(Group(0, 0))
            normalise(Group(0, 0))
            normalise_again(Group(0, 0))
            groups(dve, G, body)

        @block.scalar
        def _(act):
            for c in (ex_ok, e_ok):
                c.start(act)
            act.wait_ge(setup, SETUP)

            def body(g):
                for use in first:
                    if use[0] == "rows":
                        bank = written(act, use, g)
                        act.wait_ge(xp_ok.sem, xp_ok.done(g, 1))
                        act.wait_ge(xpr_ok.sem, xpr_ok.done(g, 1))
                        read(nc.scalar.activation(xT[:, use[1], :], bank[:, :], ACT.Copy), use)
                    elif use[0] == "up":
                        _, cp, h, e = use
                        bank = written(act, use, g)
                        read(nc.scalar.activation(up[:, cp, h, :, e, :], bank[:, :].rearrange("p (b t) -> p b t", b=NU),
                                                  ACT.Copy), use)
                act.wait_ge(lg_ok.sem, lg_ok.done(g))
                nc.scalar.activation(ex[:, :, :], lg[:, :, :], ACT.Exp).then_inc(ex_ok.sem, 1)
                for use in middle:
                    if use[0] == "u":
                        _, cp, h, e = use
                        bank = written(act, use, g)
                        read(nc.scalar.activation(uf[:, cp, h, :, e, :], bank[:, :].rearrange("p (b t) -> p b t", b=NU),
                                                  ACT.Copy), use)
                    elif use[0] == "v":
                        bank = written(act, use, g)
                        read(nc.scalar.activation(v[:, use[1], use[2], :, :, :, :].rearrange("p c e h d -> p (c e h d)"),
                                                  bank[:, :], ACT.Copy), use)
                    elif use[0] == "gates":
                        bank = written(act, use, g)
                        act.wait_ge(yn_ok.sem, yn_ok.done(g, 1))
                        read(nc.scalar.activation(gateT[:, :, :].rearrange("p b t -> p (b t)"), bank[:, :], ACT.Copy), use)
                for what, k in steps:
                    if what == "s":
                        act.wait_ge(s_ok.sem, s_ok.at(g, k + 1))
                        act.wait_ge(a_ok.sem, a_ok.at(g, k - 3))
                        nc.scalar.activation(pt[k % 4][:, :, :].rearrange("p e t -> p (e t)"), st[k % 2][:, :], ACT.Exp,
                                             scale=SCALE).then_inc(e_ok.sem, 1)
                    elif what == "proj":
                        bank = written(act, (what, k), g)
                        read(nc.scalar.activation(oT[k % 2][:, :, :].rearrange("p c t -> p (c t)"), bank[:, 0:CP * P],
                                                  ACT.Copy), (what, k))

            groups(act, G, body)

        @block.tensor
        def _(pe):
            for c in gen_ok + gen_out + [tr_ok, sn_ok, s_ok, a_ok]:
                c.start(pe)
            pe.wait_ge(consts, 16 * N_CONST)
            for j in range(EH):
                nc.tensor.matmul(sn[0][:, DC * j:DC * (j + 1)], wq[:, j, :], wk[:, j, 0:DC], start=True, stop=True)
                last = nc.tensor.matmul(sn[1][:, DC * j:DC * (j + 1)], wk[:, j, :], wq[:, j, 0:DC], start=True, stop=True)
            last.then_inc(products, 1)
            pe.wait_ge(setup, 14)
            for k in range(CP):
                last = nc.tensor.matmul(st[0][:, 0:D], pbx[:, :], owT[:, k, :], start=(k == 0), stop=(k == CP - 1))
            last.then_inc(products, 1)
            pe.wait_ge(setup, SETUP)
            pe.wait_ge(wv_in, 32)

            def bank_for(use, g):
                bank, pos = turn[use]
                pe.wait_ge(gen_out[bank].sem, gen_out[bank].at(g, pos))
                return gen[bank]

            def wrote(ins, use):
                ins.then_inc(gen_ok[turn[use][0]].sem, 1)

            def tile(t, b):
                return t[b * P:(b + 1) * P]

            def emit(use, g):
                what = use[0]
                if what == "rows":
                    if use[1] == 0:
                        pe.wait_ge(xn_ok.sem, xn_ok.done(g))
                    bank = bank_for(use, g)
                    cp = use[1]
                    for b in range(NU):
                        last = nc.tensor.transpose(bank[:, b * P:(b + 1) * P], xn[:, b, cp * P:(cp + 1) * P], ident[:, :])
                    wrote(last, use)
                elif what == "up":
                    _, cp, h, e = use
                    if (cp, h, e) == (0, 0, 0):
                        pe.sem_inc(tr_ok.sem, 1)
                        pe.wait_ge(xTr_ok.sem, xTr_ok.done(g))
                    bank = bank_for(use, g)
                    wrote(nc.tensor.matmul(bank[:, :], At[:, h * E1 + e, :], xTr[:, cp, :], start=True, stop=True), use)
                elif what == "router":
                    bank = bank_for(use, g)
                    for b in range(NU):
                        for cp in range(CP):
                            last = nc.tensor.matmul(bank[:, E1 * b:E1 * (b + 1)], xT[:, cp, b * P:(b + 1) * P],
                                                    rw[:, cp, :], start=(cp == 0), stop=(cp == CP - 1))
                    wrote(last, use)
                elif what == "u":
                    _, cp, h, e = use
                    bank = bank_for(use, g)
                    wrote(nc.tensor.matmul(bank[:, :], A[:, h * E1 + e, :], xT[:, cp, :], start=True, stop=True), use)
                elif what == "v":
                    _, b, cp = use
                    bank = bank_for(use, g)
                    wrote(nc.tensor.matmul(bank[:, :], xT[:, cp, b * P:(b + 1) * P],
                                           wv[:, :, :].rearrange("p c n -> p (c n)"), start=True, stop=True), use)
                elif what == "max":
                    pe.wait_ge(mx_ok.sem, mx_ok.at(g, 2 * CH * (use[1] + 1)))
                    bank = bank_for(use, g)
                    wrote(nc.tensor.transpose(bank[:, 0:P], mx[use[1]][:, :], ident[:, :]), use)
                elif what == "gates":
                    pe.wait_ge(ga_ok.sem, ga_ok.done(g))
                    bank = bank_for(use, g)
                    for b in range(NU):
                        last = nc.tensor.matmul(bank[:, b * P:(b + 1) * P],
                                                gate_r[:, b, :, :].rearrange("p e r -> p (e r)"), ident[:, :],
                                                start=True, stop=True)
                    wrote(last, use)
                elif what == "proj":
                    b = use[1]
                    pe.wait_ge(yn_ok.sem, yn_ok.at(g, C1 * (b + 1)))
                    bank = bank_for(use, g)
                    for cp in range(CP):
                        for h in range(NH):
                            for c in (2 * cp, 2 * cp + 1):
                                r = slice(DC * (c % 2), DC * (c % 2) + DC)
                                last = nc.tensor.matmul(bank[r, cp * P:(cp + 1) * P], wp[:, h, :],
                                                        yn[b % 2][:, c, h, :], start=(h == 0), stop=(h == NH - 1))
                    wrote(last, use)
                elif what == "fin":
                    b = use[1]
                    was_read(pe, ("proj", b), g)
                    bank = bank_for(use, g)
                    for cp in range(CP):
                        nc.tensor.matmul(bank[:, 0:D], oT[b % 2][:, cp, :], owT[:, cp, :], start=(cp == 0), stop=False)
                    wrote(nc.tensor.matmul(bank[:, 0:D], gateT[:, b, :], pbo[:, :], start=False, stop=True), use)

            def body(g):
                for use in first:
                    emit(use, g)
                pe.wait_ge(xpr_ok.sem, xpr_ok.done(g))
                for m in middle:
                    if m[0] is not None:
                        emit(m, g)
                        continue
                    k = m[1]
                    b, c, h = k // CH, k % CH // NH, k % NH
                    if b == 0 and c % 2 == 0:
                        for e in range(E1 - 2, E1):
                            was_read(pe, ("up", c // 2, h, e), g)
                    pe.wait_ge(mx_ok.sem, mx_ok.at(g, k - 1))
                    nc.tensor.matmul(sn[k % 2][:, :], xpr[0][:, c, b * P:(b + 1) * P],
                                     up[:, c // 2, h, b, :, :].rearrange("p e s -> p (e s)"), start=True, stop=True)\
                      .then_inc(sn_ok.sem, 1)
                for use in (("gates",), ("max", 1)):
                    was_read(pe, use, g)
                pe.wait_ge(xp_ok.sem, xp_ok.done(g))
                for what, k in steps:
                    if what == "s":
                        b, c, h = k // CH, k % CH // NH, k % NH
                        if k % (2 * CH) == 0:
                            pe.wait_ge(row_in[b // 2], g.n * 32 + 32)
                        pe.wait_ge(e_ok.sem, e_ok.at(g, k - 1))
                        nc.tensor.matmul(st[k % 2][:, :], xp[g.u][:, c, b * P:(b + 1) * P],
                                         uf[:, c // 2, h, b, :, :].rearrange("p e s -> p (e s)"), start=True, stop=False)
                        nc.tensor.matmul(st[k % 2][:, :], pick[:, k % CH, :], mrow[:, b, :], start=False, stop=True)\
                          .then_inc(s_ok.sem, 1)
                    elif what == "a":
                        b, c, h, j = k // CH, k % CH // NH, k % NH, k // 2
                        pe.wait_ge(e_ok.sem, e_ok.at(g, k + 1))
                        pe.wait_ge(yn_ok.sem, yn_ok.at(g, j - 1))
                        for row, part in ((0, None), (1, ones)):
                            for e in range(E1):
                                lhsT = v[:, b, c // 2, c % 2, e, h, :] if part is None else ones[:, :]
                                last = nc.tensor.matmul(av[j % 2][R * e:R * (e + 1), row, h, :], lhsT, pt[k % 4][:, e, :],
                                                        start=True, stop=True)
                        last.then_inc(a_ok.sem, 1)
                    else:
                        emit((what, k), g)

            groups(pe, G, body)


def program(nc, io, out):
    with ExitStack() as ctx:
        keep = {
            "slot": ctx.enter_context(nc.sbuf_tensor("slot_of_token", [P, GRAPHS], U32)),
            "gate": ctx.enter_context(nc.sbuf_tensor("gate_of_token", [P, GRAPHS], F32)),
        }
        dram = {
            "x1": nc.dram_tensor("x1_rows", (T, D), F32, kind="Internal").ap(),
            "x1n": nc.dram_tensor("x1n_rows", (T, D), F32, kind="Internal").ap(),
            "slot_token": nc.dram_tensor("token_of_slot", (SLOTS + T, 1), U32, kind="Internal").ap(),
            "y": nc.dram_tensor("expert_rows", (SLOTS, D), F32, kind="Internal").ap(),
        }
        dram["x3"] = nc.dram_tensor("x3_rows", (T, D), F32, kind="Internal").ap()
        graph_block_0(nc, io, dram, keep)
        experts(nc, io, dram)
        graph_block_1(nc, io, dram, keep)
        attention(nc, io, dram, out)


def kernel(**inputs):
    import numpy as np
    import concourse.bacc as bacc
    from concourse.bass_utils import run_bass_kernel_spmd

    i = {k: np.ascontiguousarray(v) for k, v in inputs.items()}

    def rows(v):
        return np.broadcast_to(v.reshape(1, -1), (P, v.size))

    def column(v):
        return v.reshape(-1, P).T

    f32 = np.float32
    qkv = i["L1_ffn_qkv_w"].reshape(E1, 3, NH, DH, DC)
    twice = (2, 1)

    def by_head(w):
        w = w.transpose(2, 1, 0, 3)[:, :, :, None, :]
        return np.broadcast_to(w, (DH, NH, E1, 2, DC)).reshape(DH, -1)

    lay = {
        "x": i["x"].reshape(T, D),
        "adjT": i["adj"].transpose(0, 2, 1).reshape(T, P),
        "eps0": rows(i["L0_gnn_eps"]),
        "W1a": i["L0_gnn_W1"], "b1a": column(i["L0_gnn_b1"]),
        "W2a": i["L0_gnn_W2"], "b2a": rows(i["L0_gnn_b2"]),
        "gate_w": i["L0_ffn_gate_w"], "gate_b": rows(i["L0_ffn_gate_b"]),
        "ew1": i["L0_ffn_w1"], "ew2": i["L0_ffn_w2"],
        "eb1": i["L0_ffn_b1"].reshape(E0, F0 // P, P).transpose(0, 2, 1),
        "eb2": np.broadcast_to(i["L0_ffn_b2"][:, None, :], (E0, P, D)),
        "eps1": rows(i["L1_gnn_epsilon"].reshape(1)),
        "W1c": i["L1_gnn_W1"], "b1c": column(i["L1_gnn_b1"]), "rms_w": column(i["L1_gnn_rms_weight"]),
        "W2c": i["L1_gnn_W2"], "b2c": rows(i["L1_gnn_b2"]),
        "norm_w": rows(i["L1_ffn_norm_w"]),
        "router_w": i["L1_ffn_router_w"].T, "router_b": rows(i["L1_ffn_router_b"]),
        "wq": by_head(qkv[:, 0]), "wk": by_head(qkv[:, 1]),
        "wv": qkv[:, 2].transpose(3, 0, 1, 2).reshape(DC, DC * E1),
        "wp": i["L1_ffn_proj_w"].reshape(E1, DC, NH, DH).transpose(0, 3, 2, 1).reshape(P, NH * DC),
        "pb": np.tile(i["L1_ffn_proj_b"].T, twice),
        "owT": i["L1_ffn_out_w"].T,
        "ident": np.eye(P, dtype=f32),
        "tri": np.triu(np.ones((P, P), f32)),
        "iota_e": rows(np.arange(E0, dtype=f32)),
        "tok": (np.arange(P)[:, None] + P * np.arange(NU)[None, :]).astype(f32),
        "no_token": np.zeros((P, (SLOTS + T) // P), np.uint32),
        "pick": np.repeat(np.eye(P, CH, dtype=f32)[:, :, None], P, axis=2).reshape(P, CH * P),
    }
    nc = bacc.Bacc("TRN2", target_bir_lowering=False, num_devices=1)
    io, arrays = {}, {}
    for name, a in lay.items():
        a = np.ascontiguousarray(a)
        arrays["in_" + name] = a
        io[name] = nc.dram_tensor("in_" + name, a.shape, mybir.dt.from_np(a.dtype), kind="ExternalInput").ap()
    out = nc.dram_tensor("out_rows", (T, D), F32, kind="ExternalOutput").ap()
    program(nc, io, out)
    r = run_bass_kernel_spmd(nc, [arrays], core_ids=[0])
    return r.results[0]["out_rows"].reshape(GRAPHS, P, D)
```
